# Optimizing a Trainium2 kernel written in Bass

```python
import numpy as np
import jax
import jax.numpy as jnp

def _softmax(x, axis=-1):
    return jax.nn.softmax(x, axis=axis)

def _gelu(x):
    return jax.nn.gelu(x, approximate=True)

def _silu(x):
    return jax.nn.silu(x)

def _sigmoid(x):
    return jax.nn.sigmoid(x)

def _layernorm(x, axis=-1, eps=1e-05):
    m = jnp.mean(x, axis=axis, keepdims=True)
    v = jnp.var(x, axis=axis, keepdims=True)
    return (x - m) / jnp.sqrt(v + eps)

def _scatter_add(tgt, idx, src, axis=0):
    return tgt.at[idx].add(src)

def _segment_sum(src, seg, n):
    return jax.ops.segment_sum(src, seg, n)
kernel_name = 'mk_recurrent_d1_jaxref_r2_63b9a3'

def setup_inputs(seed: int=0):
    np.random.seed(seed)
    _w = jnp.asarray

    def _L0_attn_setup():
        import jax, jax.numpy as jnp
        import numpy as np
        import math
        B, L, D, N = (8, 2048, 512, 16)
        key = jax.random.key(seed)
        k1, k2, k3, k4, k5, k6 = jax.random.split(key, 6)
        return {'x': jax.random.normal(k1, (B, L, D), dtype=jnp.float32), 'delta': jax.random.normal(k2, (D, N, 1), dtype=jnp.float32), 'alpha': jax.random.normal(k3, (D, N, 1), dtype=jnp.float32), 'beta': jax.random.normal(k4, (D, N, 1), dtype=jnp.float32), 'gamma': jax.random.normal(k5, (D, N), dtype=jnp.float32), 'omega': jax.random.normal(k6, (D,), dtype=jnp.float32)}
    _L0_attn_in = _L0_attn_setup()

    def _L0_ffn_setup():
        import jax, jax.numpy as jnp
        import numpy as np
        D_MODEL = 512
        NUM_EXPERTS = 8
        TOP_K = 2
        key = jax.random.key(seed)
        ks = jax.random.split(key, 5)
        scale = 1.0 / np.sqrt(D_MODEL)
        x = jax.random.normal(ks[0], (4, 1024, D_MODEL), dtype=jnp.float32)
        We = jax.random.uniform(ks[1], (NUM_EXPERTS, D_MODEL, D_MODEL), jnp.float32, -scale, scale)
        be = jax.random.uniform(ks[2], (NUM_EXPERTS, D_MODEL), jnp.float32, -scale, scale)
        Wg = jax.random.uniform(ks[3], (NUM_EXPERTS, D_MODEL), jnp.float32, -scale, scale)
        bg = jax.random.uniform(ks[4], (NUM_EXPERTS,), jnp.float32, -scale, scale)
        return {'x': x, 'We': We, 'be': be, 'Wg': Wg, 'bg': bg}
    _L0_ffn_in = _L0_ffn_setup()
    _d = {'L0_attn_x': _L0_attn_in['x'], 'L0_attn_delta': _L0_attn_in['delta'], 'L0_attn_alpha': _L0_attn_in['alpha'], 'L0_attn_beta': _L0_attn_in['beta'], 'L0_attn_gamma': _L0_attn_in['gamma'], 'L0_attn_omega': _L0_attn_in['omega'], 'L0_ffn_We': _L0_ffn_in['We'], 'L0_ffn_be': _L0_ffn_in['be'], 'L0_ffn_Wg': _L0_ffn_in['Wg'], 'L0_ffn_bg': _L0_ffn_in['bg']}
    _x0 = _d['L0_attn_x']
    _d['L0_attn_x'] = jax.random.normal(jax.random.fold_in(jax.random.key(seed), 1), (2, 4096, 512), dtype=_x0.dtype)
    del _x0
    return _d

def reference(L0_attn_x, L0_attn_delta, L0_attn_alpha, L0_attn_beta, L0_attn_gamma, L0_attn_omega, L0_ffn_We, L0_ffn_be, L0_ffn_Wg, L0_ffn_bg):

    def _L0_attn_ref(x, delta, alpha, beta, gamma, omega):
        import jax, jax.numpy as jnp
        import numpy as np
        import math
        B, L, D, N = (8, 2048, 512, 16)
        b, l, d = x.shape
        n_state = gamma.shape[-1]
        scale = math.sqrt(1.0 / n_state)
        residual = x * omega
        xt = jnp.swapaxes(x, -1, -2)
        p = jax.nn.sigmoid(delta)
        a = jax.nn.sigmoid(alpha)
        q = 1.0 - p * a
        t = jnp.arange(l, dtype=x.dtype)
        vander = t[None, None, :] * jnp.log(q)
        kernel = p * beta * jnp.exp(vander)
        k = jnp.einsum('dnl,dn->dl', kernel, gamma * scale)
        n_fft = 2 * l
        k_f = jnp.fft.rfft(k, n=n_fft)
        x_f = jnp.fft.rfft(xt, n=n_fft)
        out = jnp.fft.irfft(x_f * k_f, n=n_fft)[..., :l]
        return jnp.swapaxes(out, -1, -2) + residual

    def _L0_ffn_ref(x, We, be, Wg, bg):
        import jax, jax.numpy as jnp
        import numpy as np
        D_MODEL = 512
        NUM_EXPERTS = 8
        TOP_K = 2
        B, S, D = x.shape
        xf = x.reshape(-1, D)
        gate_logits = xf @ Wg.T + bg
        topk_vals, topk_idx = jax.lax.top_k(gate_logits, TOP_K)
        gate_w = jax.nn.softmax(topk_vals, axis=-1)
        all_out = jnp.einsum('nd,ehd->neh', xf, We) + be
        sel = jnp.take_along_axis(all_out, topk_idx[:, :, None], axis=1)
        out = jnp.sum(sel * gate_w[:, :, None], axis=1)
        return out.reshape(B, S, D)
    x = L0_attn_x
    xn = _layernorm(x, axis=-1)
    s = _L0_attn_ref(xn, L0_attn_delta, L0_attn_alpha, L0_attn_beta, L0_attn_gamma, L0_attn_omega)
    g = _silu(_L0_ffn_ref(xn, L0_ffn_We, L0_ffn_be, L0_ffn_Wg, L0_ffn_bg))
    x = x + s * g
    return x

_drawn_inputs = setup_inputs


def setup_inputs(seed=0):
    import zlib

    import numpy as np

    out = dict(_drawn_inputs(seed))
    spreads = {}
    factors = {'L0_ffn_be': 4.592}
    for name, (base, spread) in spreads.items():
        noise = np.random.default_rng([zlib.crc32(name.encode()), seed]).standard_normal(out[name].shape)
        drawn = base * np.exp(spread * noise) if base else spread * noise
        out[name] = jnp.asarray(drawn.astype(out[name].dtype))
    for name, factor in factors.items():
        out[name] = (out[name] * factor).astype(out[name].dtype)
    return out
```

```python
import concourse.bass as bass
from concourse import mybir
from contextlib import ExitStack

P = 128
D = 512
NB = 2
NT = 64
TPB = NT // NB
NS = 16
GC = P // NS
NG = D // GC
NQ = 4
GPQ = NG // NQ
NE = 8
NPAIR = NE * (NE - 1) // 2
NX = NT + NPAIR
TF = 8
EPS = 1e-5

C_ID, C_TRI, C_MASK, C_DESC, C_PAIR, C_DA, C_DB, C_ONE, C_E0, C_E1, C_IOTA = (
    0, 128, 256, 264, 272, 300, 328, 356, 357, 358, 359)
NCST = 360


def program(nc, x, delta, alpha, beta, gamma, omega, weT, be, wgT, bg, cst, tok, out):
    f32, i32, bf16 = mybir.dt.float32, mybir.dt.int32, mybir.dt.bfloat16
    ALU, ACT, AX = mybir.AluOpType, mybir.ActivationFunctionType, mybir.AxisListType
    with ExitStack() as ctx:
        def sb(name, shape, dt=f32):
            return ctx.enter_context(nc.sbuf_tensor(name, shape, dt))

        def sem(name):
            return ctx.enter_context(nc.semaphore(name))

        kr = nc.dram_tensor("kr", [D, 2 * P], f32, kind="Internal").ap()
        s_dram = nc.dram_tensor("s_rows", [NT * P, D], f32, kind="Internal").ap()
        table = nc.dram_tensor("slot_table", [NX * P, TF], f32, kind="Internal").ap()
        x_rows = x.rearrange("b l d -> (b l) d")
        out_rows = out.rearrange("b l d -> (b l) d")

        XN = sb("XN", [P, NQ, NT, P])
        R = sb("R", [P, NG, P])
        Tb = sb("Tb", [P, 2, GC, P])
        Xg = sb("Xg", [P, 2, GC, NT])
        Rg = sb("Rg", [P, 4, P])
        V = sb("V", [P, 2, P])
        rhs2 = sb("rhs2", [P, 2, GC, NT])
        SC = sb("SC", [P, 2, NB, TPB + 1])
        ST = sb("ST", [P, 2, NT])
        maskcq = sb("maskcq", [P, NG, GC])
        C = sb("C", [P, NCST])
        tri16 = sb("tri16", [P, P], bf16)
        ones16 = sb("ones16", [P, P], bf16)
        wg = sb("wg", [P, NQ, NE])
        bgs = sb("bgs", [P, NE])
        om8 = sb("om8", [GC, NG])
        small = sb("small", [P, 14, NG])
        PW, SG, QP = small[:, 0:4], small[:, 4:6], small[:, 6:14]
        SLF = small[:, 12]
        ra = small[:, 0:8]
        pr28 = small[:, 8:12].rearrange("p a b -> p (a b)")[:, 0:8 * NPAIR].rearrange("p (a r) -> p a r", r=NPAIR)
        RT = sb("RT", [P, NPAIR * NT])
        CNT = sb("CNT", [P, NPAIR, NT], bf16)
        RB = sb("RB", [P, 1376])
        TOK = sb("TOK", [P, NT, TF])
        SLOT = sb("SLOT", [P, NT], i32)
        AB = sb("AB", [P, 2])
        EO = sb("EO", [1, 2 * P], i32)
        bst = sb("bst", [P, 4, 6])
        mv = sb("mv", [P, 4, 2])
        ve, sd, r0, r1 = sb("ve", [P, 2, 2]), sb("sd", [P, 2, 2]), sb("r0", [P, 2, 2]), sb("r1", [P, 2, 2])
        rs = sb("rs", [P, 2, 2])
        carrier = sb("carrier", [1, 1])
        pay = sb("pay", [P, 8, TF])
        six = sb("six", [P, 8], i32)
        gix = sb("gix", [P, 4, 2], i32)
        oix = sb("oix", [P, 4, 1], i32)

        xnb = [rhs2[:, u].rearrange("p a b -> p (a b)") for u in range(2)]
        xnT = [RT[:, u * D:(u + 1) * D] for u in range(2)]
        cmask = RT[:, 2 * D:3 * D].rearrange("p (g d) -> p g d", d=GC)
        LG = RT[:, 0:D].rearrange("p (t e) -> p t e", e=NE)
        LQ = RT[:, D:2 * D].rearrange("p (t e) -> p t e", e=NE)
        LR = RT[:, 2 * D:3 * D].rearrange("p (t e) -> p t e", e=NE)
        SCAN = RT[:, :].rearrange("p (r t) -> p r t", t=NT)
        tab0 = CNT[:, :, :].rearrange("p r t -> p (r t)")[:, 0:2 * NX * TF].bitcast(f32)
        kS = [RB[0:GC, u * D:(u + 1) * D].rearrange("p (g j) -> p g j", g=4) for u in range(2)]
        cmg = RT[:, 3 * D:3 * D + 8 * GC].rearrange("p (u g d) -> p u g d", u=2, d=GC)
        OH = RB[:, 0:NPAIR * NT // 2].bitcast(bf16).rearrange("p (t r) -> p t r", r=NPAIR)
        TMP = RB[:, NPAIR * NT // 2:NPAIR * NT // 2 + NPAIR * 16].rearrange("p (t r) -> p t r", r=NPAIR)

        W = XN[:, 0:2].rearrange("p q t d -> p (q t d)").rearrange("p (c e h) -> p c e h", c=NQ, e=NE)
        late = XN[:, 2:4].rearrange("p q t d -> p (q t d)")
        BE = late[:, 0:NE * D].rearrange("p (e h) -> p e h", e=NE)
        place = [NE * D]

        def lane(n, width=D):
            at = [late[:, place[0] + i * width:place[0] + (i + 1) * width] for i in range(n)]
            place[0] += n * width
            return at
        xg, sg, og = lane(4), lane(4), lane(4)
        xm, xmT, uu, tt, gg = lane(2), lane(2), lane(2), lane(2), lane(2)
        TB = lane(1, NX * TF)[0].rearrange("p (i f) -> p i f", f=TF)

        bank = [ctx.enter_context(nc.psum_tensor(f"bank{i}", [P, D], f32)) for i in range(8)]
        pLG = bank[6][:, :].rearrange("p (t e) -> p t e", e=NE)

        s_const, s_be, s_tab, s_w = sem("s_const"), sem("s_be"), sem("s_tab"), sem("s_w")
        s_sig = sem("s_sig")
        s_taps = sem("s_taps")
        cm_ready, pk_done, ks_ev, ks_om = sem("cm_ready"), sem("pk_done"), sem("ks_ev"), sem("ks_om")
        ks_out = [sem("ks_out0"), sem("ks_out1")]
        x_in = [sem("x_in0"), sem("x_in1")]
        st_ready, sd_ready, rs_ready, xn_norm = sem("st_ready"), sem("sd_ready"), sem("rs_ready"), sem("xn_norm")
        tk_copied = sem("tk_copied")
        xn_copied, xT_done, xT_ev, gate_done = sem("xn_copied"), sem("xT_done"), sem("xT_ev"), sem("gate_done")
        rg_ready, xg_ready, vt_done, v_ev = sem("rg_ready"), sem("xg_ready"), sem("vt_done"), sem("v_ev")
        s1_done, s_ext, rhs2_ready = sem("s1_done"), sem("s_ext"), sem("rhs2_ready")
        t_in = [sem("t_in0"), sem("t_in1")]
        t_done, s2_done, o_ev = sem("t_done"), sem("s2_done"), sem("o_ev")
        s_out = [sem(f"s_out{q}") for q in range(NQ)]
        lg_read, m_ready, e_ready, oh_ready = sem("lg_read"), sem("m_ready"), sem("e_ready"), sem("oh_ready")
        cnt_done, cnt_ev, pre_done, pre_ev = sem("cnt_done"), sem("cnt_ev"), sem("pre_done"), sem("pre_ev")
        slot_ready, ab_ready, eo_done, eo_ready = sem("slot_ready"), sem("ab_ready"), sem("eo_done"), sem("eo_ready")
        pay_ready, sc_done = sem("pay_ready"), sem("sc_done")
        g_ix, gx, gs = sem("g_ix"), [sem(f"gx{b}") for b in range(4)], [sem(f"gs{b}") for b in range(4)]
        o_ix, o_out = sem("o_ix"), [sem(f"o_out{b}") for b in range(4)]
        xm_ready, x3_done, x3_ev, mm_done = sem("xm_ready"), sem("x3_done"), sem("x3_ev"), sem("mm_done")
        t_ready, g_ready, o_ready = sem("t_ready"), sem("g_ready"), sem("o_ready")

        block = ctx.enter_context(nc.Block())

        def col(c, n=1):
            return C[:, c:c + n]

        def need(eng, semaphore, value):
            if not isinstance(value, int) or value > 0:
                eng.wait_ge(semaphore, value)

        def looped(eng, lo, hi, body, peel=1):
            for i in range(lo, lo + peel):
                body(i)
            if hi > lo + peel:
                with eng.Fori(lo + peel, hi) as i:
                    body(i)

        @block.sync
        def _(sp):
            sp.dma_start(C[:], cst).then_inc(s_const, 16)
            for k, a in enumerate((delta, alpha, beta, gamma)):
                sp.dma_start(PW[:, k, :], a).then_inc(s_const, 16)
            sp.dma_start(om8[:], omega).then_inc(s_const, 16)
            sp.dma_start(wg[:], wgT).then_inc(s_const, 16)
            sp.dma_start(bgs[:], bg.partition_broadcast(P)).then_inc(s_const, 16)
            sp.dma_start(TOK[:].bitcast(i32), tok).then_inc(s_const, 16)

            x_pairs = x_rows.rearrange("(t p) (q d) -> p q t d", p=P, q=NQ)

            for u in range(2):
                for q in range(NQ):
                    sp.dma_start(XN[:, q, 2 * u:2 * u + 2, :], x_pairs[:, q, 2 * u:2 * u + 2, :]).then_inc(x_in[u], 16)
            sp.wait_ge(s_taps, 1)
            for u in range(2):
                sp.dma_start(kr[u * 256:(u + 1) * 256, P:2 * P].rearrange("(a p) j -> p a j", p=P),
                             rhs2[:, 1, 0:4, :].rearrange("p a b -> p (a b)").rearrange("p (a j) -> p a j", a=2)
                             ).then_inc(ks_out[u], 16)
            sp.dma_start(table.rearrange("(p i) f -> p (i f)", p=P), tab0).then_inc(s_tab, 16)
            kr_g = kr.rearrange("(g d) j -> d g j", d=GC)
            with sp.Fori(0, 8) as i:
                for u in range(2):
                    sp.wait_ge(ks_om, i * 2 + (u + 1))
                    sp.dma_start(kr_g[:, bass.ds(i * 8 + 4 * u, 4), 0:P], kS[u]).then_inc(ks_out[u], 16)
            with sp.Fori(1, NT // 4) as i:
                for u in range(2):
                    sp.wait_ge(x_in[u], i * 64)
                    for q in range(NQ):
                        sp.dma_start(XN[:, q, bass.ds(i * 4 + 2 * u, 2), :],
                                     x_pairs[:, q, bass.ds(i * 4 + 2 * u, 2), :]).then_inc(x_in[u], 16)
            for u in range(2):
                sp.wait_ge(ks_out[u], 16 * 9)
            kr_t = bass.AP(kr.tensor, 0, [[1, P], [2 * P, D], [1, P]])

            def blocks(i):
                for r in range(2):
                    g = i * 2 + r
                    need(sp, t_done, g - 1)
                    sp.dma_start(Tb[:, r], kr_t[:, bass.ds(g * GC, GC), :]).then_inc(t_in[r], 16)

            s_view = s_dram.rearrange("(t p) d -> p t d", p=P)

            def store_s(q):
                sp.wait_ge(o_ev, GPQ * (q + 1))
                sp.dma_start(s_view[:, :, q * P:(q + 1) * P], XN[:, q]).then_inc(s_out[q], 16)

            for q in range(NQ):
                looped(sp, GPQ // 2 * q, GPQ // 2 * (q + 1), blocks)
                if q > 0:
                    store_s(q - 1)
                if q == 2:
                    sp.wait_ge(s_out[0], 16)
                    sp.wait_ge(s_out[1], 16)
                    sp.dma_start(W, weT).then_inc(s_w, 16)
            store_s(3)
            sp.wait_ge(s_out[2], 16)
            sp.dma_start(BE, be.rearrange("e h -> (e h)").partition_broadcast(P).rearrange("p (e h) -> p e h", e=NE)
                         ).then_inc(s_be, 16)
            sp.wait_ge(s_out[3], 16)
            sp.wait_ge(sc_done, 16 * NT)
            sp.dma_start(TB, table.rearrange("(i p) f -> p i f", p=P)).then_inc(s_tab, 16)

        @block.gpsimd
        def _(pool):
            pool.wait_ge(s_const, 16 * 9)

            def norm(i):
                for u in range(2):
                    n = i * 2 + u
                    pool.wait_ge(rs_ready, n + 1)
                    nc.gpsimd.tensor_copy(TOK[:, bass.ds(n * 2, 2), 4], mv[:, 2 * u:2 * u + 2, 0]).then_inc(tk_copied, 1)
                    nc.gpsimd.tensor_copy(TOK[:, bass.ds(n * 2, 2), 5], rs[:, u]).then_inc(tk_copied, 1)
                    for k in range(2):
                        t = i * 4 + (2 * u + k)
                        pool.wait_ge(xn_norm, t + 1)
                        nc.gpsimd.tensor_copy(
                            XN[:, :, bass.ds(t, 1), :].rearrange("p q o d -> p q (o d)"),
                            xnb[k].rearrange("p (q d) -> p q d", q=NQ)).then_inc(xn_copied, 1)
            looped(pool, 0, NT // 4, norm)
            pool.wait_ge(xn_copied, NT)

            def then_dma():
                nc.gpsimd.tensor_tensor(carrier[:], C[0:1, 0:1], C[0:1, 0:1], ALU.add)

            def feed(q, i):
                for k in range(4):
                    g = i * 4 + (GPQ * q + k)
                    need(pool, s2_done, g - 3)
                    nc.gpsimd.tensor_copy(Rg[:, k], R[:, bass.ds(g, 1), :].rearrange("p o j -> p (o j)")
                                          ).then_inc(rg_ready, 1)
                    need(pool, t_done, g - 1)
                    nc.gpsimd.tensor_copy(
                        Xg[:, k % 2],
                        XN[:, q, :, bass.ds(i * 32 + 8 * k, GC)].rearrange("p t d -> p d t")).then_inc(xg_ready, 1)

            def scatter(i):
                for k in range(8):
                    t = i * 8 + k
                    nc.gpsimd.tensor_copy(pay[:, k].bitcast(i32), TOK[:, bass.ds(t, 1), :].rearrange("p o f -> p (o f)").bitcast(i32))
                    nc.gpsimd.tensor_copy(six[:, k:k + 1], SLOT[:, bass.ds(t, 1)]).then_inc(pay_ready, 1)
                    pool.wait_ge(pay_ready, t + 1)
                    then_dma()
                    nc.gpsimd.indirect_dma_start(
                        out=table, out_offset=bass.IndirectOffsetOnAxis(ap=six[:, k:k + 1], axis=0),
                        in_=pay[:, k], in_offset=None).then_inc(sc_done, 16)

            for q in range(NQ):
                if q == 2:
                    pool.wait_ge(slot_ready, 1)
                    pool.wait_ge(s_tab, 16)

                def fed(i):
                    if q >= 2:
                        scatter(i + 4 * (q - 2))
                    feed(q, i)
                    if q >= 2:
                        pool.wait_ge(sc_done, (i + 4 * (q - 2)) * 128 + 128)
                looped(pool, 0, 4, fed)

            pool.wait_ge(s_tab, 32)
            for b in range(4):
                nc.gpsimd.memset(xg[b], 0.0)
                last = nc.gpsimd.memset(sg[b], 0.0)
            last.then_inc(g_ix, 1)
            pool.wait_ge(g_ix, 1)

            def gather(b, n):
                nc.gpsimd.tensor_copy(gix[:, b], TB[:, bass.ds(n, 1), 0:2].bitcast(i32).rearrange("p o f -> p (o f)")
                                      ).then_inc(g_ix, 1)
                pool.wait_ge(g_ix, n + 2)
                then_dma()
                nc.gpsimd.indirect_dma_start(
                    out=xg[b], out_offset=None, in_=x_rows,
                    in_offset=bass.IndirectOffsetOnAxis(ap=gix[:, b, 0:1], axis=0),
                    bounds_check=NT * P - 1, oob_is_err=False).then_inc(gx[b], 16)
                nc.gpsimd.indirect_dma_start(
                    out=sg[b], out_offset=None, in_=s_dram,
                    in_offset=bass.IndirectOffsetOnAxis(ap=gix[:, b, 1:2], axis=0),
                    bounds_check=NT * P - 1, oob_is_err=False).then_inc(gs[b], 16)

            def give(b, n):
                nc.gpsimd.tensor_copy(oix[:, b], TB[:, bass.ds(n, 1), 0:1].bitcast(i32).rearrange("p o f -> p (o f)")
                                      ).then_inc(o_ix, 1)
                pool.wait_ge(o_ix, n + 1)
                pool.wait_ge(o_ready, n + 1)
                then_dma()
                nc.gpsimd.indirect_dma_start(
                    out=out_rows, out_offset=bass.IndirectOffsetOnAxis(ap=oix[:, b, 0:1], axis=0),
                    in_=og[b], in_offset=None,
                    bounds_check=NT * P - 1, oob_is_err=False).then_inc(o_out[b], 16)

            for n in range(3):
                gather(n, n)

            def steps(i):
                for k in range(4):
                    gather((k + 3) % 4, i * 4 + (k + 3))
                    give(k, i * 4 + k)
            looped(pool, 0, NX // 4 - 1, steps)
            for k in range(4):
                n = NX - 4 + k
                if n + 3 < NX:
                    gather((k + 3) % 4, n + 3)
                give(k, n)
            for b in range(4):
                pool.wait_ge(o_out[b], 16 * (NX // 4))

        @block.scalar
        def _(act):
            act.wait_ge(s_const, 16 * 9)
            nc.scalar.activation(SG, PW[:, 0:2], ACT.Sigmoid).then_inc(s_sig, 1)

            def taps(i):
                for u in range(2):
                    act.wait_ge(pk_done, i * 2 + (u + 1))
                    act.wait_ge(ks_out[u], i * 16 + 16)
                    nc.scalar.activation(kS[u], bank[2 + u][0:GC, :].rearrange("p (g j) -> p g j", g=4),
                                         ACT.Copy).then_inc(ks_ev, 1)
            looped(act, 0, 8, taps)

            def root(n, u):
                act.wait_ge(st_ready, n + 1)
                nc.scalar.activation(sd[:, u], ve[:, u], ACT.Sqrt).then_inc(sd_ready, 1)

            def xt(i):
                for k in range(4):
                    t = i * 4 + k
                    if k % 2 == 0 and not (isinstance(i, int) and i == NT // 4 - 1 and k == 2):
                        root(i * 2 + (k // 2 + 1), (k // 2 + 1) % 2)
                    act.wait_ge(xT_done, t + 1)
                    need(act, gate_done, t - 1)
                    nc.scalar.activation(xnT[k % 2], bank[k % 2][:, :], ACT.Copy).then_inc(xT_ev, 1)
            root(0, 0)
            looped(act, 0, NT // 4 - 1, xt)
            xt(NT // 4 - 1)

            def v_out(b, g):
                act.wait_ge(vt_done, g + 1)
                need(act, s1_done, g - 1)
                nc.scalar.activation(V[:, b], bank[b][:, 0:P], ACT.Copy).then_inc(v_ev, 1)

            def s_back(q, i, k):
                act.wait_ge(s2_done, i * 4 + (GPQ * q + k + 1))
                nc.scalar.activation(
                    XN[:, q, :, bass.ds(i * 32 + 8 * k, GC)],
                    bank[4 + k % 2][:, :].rearrange("p (d t) -> p t d", d=GC), ACT.Copy).then_inc(o_ev, 1)

            v_out(0, 0)
            for q in range(NQ):
                def conv(i):
                    for k in range(4):
                        v_out((k + 1) % 2, i * 4 + (GPQ * q + k + 1))
                        s_back(q, i, k)
                looped(act, 0, 4 if q < NQ - 1 else 3, conv)
                if q == 0:
                    act.wait_ge(m_ready, 1)
                    nc.scalar.activation(ra[:, 4, :], ra[:, 3, :], ACT.Exp).then_inc(e_ready, 1)
            for k in range(4):
                if k < 3:
                    v_out((k + 1) % 2, NG - 4 + k + 1)
                s_back(NQ - 1, 3, k)

            def xt3(b, n):
                act.wait_ge(x3_done, n + 1)
                need(act, mm_done, n - 1)
                nc.scalar.activation(xmT[b], bank[b][:, :], ACT.Copy).then_inc(x3_ev, 1)

            def silu(b, n):
                act.wait_ge(t_ready, n + 1)
                need(act, o_ready, n - 1)
                nc.scalar.activation(gg[b], tt[b], ACT.Silu).then_inc(g_ready, 1)

            xt3(0, 0)

            def steps(i):
                for k in range(4):
                    xt3((k + 1) % 2, i * 4 + (k + 1))
                    silu(k % 2, i * 4 + k)
            looped(act, 0, NX // 4 - 1, steps)
            for k in range(4):
                if k < 3:
                    xt3((k + 1) % 2, NX - 4 + k + 1)
                silu(k % 2, NX - 4 + k)

        @block.vector
        def _(v):
            V_ = nc.vector
            v.wait_ge(s_const, 16 * 9)
            V_.memset(rhs2[:, 1], 0.0)
            V_.memset(SC[:], 0.0)
            V_.memset(ones16[:], 1.0)
            V_.tensor_copy(tri16[:], col(C_TRI, P))
            V_.memset(tab0, 0.0)
            v.drain()
            V_.memset(tab0.rearrange("p (i f) -> p i f", f=TF)[:, :, 0:2].bitcast(i32), NT * P)
            v.wait_ge(s_sig, 1)
            V_.tensor_tensor(PW[:, 0], SG[:, 0], SG[:, 1], ALU.mult)
            V_.tensor_tensor(PW[:, 1], SG[:, 0], PW[:, 2], ALU.mult)
            v.drain()
            V_.tensor_scalar(QP[:, 0], PW[:, 0], -1.0, 1.0, ALU.mult, ALU.add)
            V_.scalar_tensor_tensor(out=PW[:, 2], in0=PW[:, 3], scalar=NS ** -0.5, in1=PW[:, 1],
                                    op0=ALU.mult, op1=ALU.mult)
            v.drain()
            V_.tensor_tensor(PW[:, 3], PW[:, 2], QP[:, 0], ALU.mult)
            for k in range(7):
                V_.tensor_tensor(QP[:, k + 1], QP[:, k], QP[:, k], ALU.mult)
                v.drain()
            V_.memset(R[:, :, P - 1:P], 1.0)
            v.drain()
            for k in range(7):
                w = 1 << k
                V_.tensor_tensor(R[:, :, P - 2 * w:P - w], R[:, :, P - w:P],
                                 QP[:, k].unsqueeze(2).to_broadcast([P, NG, w]), ALU.mult)
                v.drain()
            mask = col(C_MASK, GC).unsqueeze(1).to_broadcast([P, NG, GC])
            V_.tensor_tensor(cmask, mask, PW[:, 2].unsqueeze(2).to_broadcast([P, NG, GC]), ALU.mult)
            V_.tensor_tensor(maskcq[:], mask, PW[:, 3].unsqueeze(2).to_broadcast([P, NG, GC]), ALU.mult)
            v.drain().then_inc(s_taps, 1)

            def cm(u, j):
                V_.tensor_copy(cmg[:, u], cmask[:, bass.ds(j * 4, 4), :]).then_inc(cm_ready, 1)
            cm(0, 0)
            cm(1, 1)

            def taps(i, last):
                for u in range(2):
                    v.wait_ge(ks_ev, i * 2 + (u + 1))
                    V_.tensor_tensor(kS[u][:, :, P - 1:P], kS[u][:, :, P - 1:P],
                                     om8[:, bass.ds(i * 8 + 4 * u, 4)].unsqueeze(2), ALU.add).then_inc(ks_om, 1)
                    if not last:
                        cm(u, i * 2 + (2 + u))
            with v.Fori(0, 7) as i:
                taps(i, False)
            taps(7, True)

            v.wait_ge(ks_out[0], 16)
            v.wait_ge(ks_out[1], 16)

            def stats(n, u, i):
                v.wait_ge(x_in[u], i * 64 + 64)
                need(v, tk_copied, n * 2 - 2)
                for k in range(2):
                    V_.bn_stats(bst[:, 2 * u + k],
                                XN[:, :, bass.ds(n * 2 + k, 1), :].rearrange("p q o d -> p q (o d)"))
                v.drain()
                for k in range(2):
                    V_.bn_aggr(mv[:, 2 * u + k], bst[:, 2 * u + k])
                v.drain()
                V_.tensor_scalar(ve[:, u], mv[:, 2 * u:2 * u + 2, 1], EPS, None, ALU.add).then_inc(st_ready, 1)

            def invert(n, u):
                v.wait_ge(sd_ready, n + 1)
                V_.reciprocal(r0[:, u], sd[:, u])
                v.drain()
                V_.tensor_tensor(r1[:, u], r0[:, u], r0[:, u], ALU.mult)
                v.drain()
                V_.scalar_tensor_tensor(out=r1[:, u], in0=r1[:, u], scalar=-0.5, in1=ve[:, u],
                                        op0=ALU.mult, op1=ALU.mult)
                v.drain()
                need(v, tk_copied, n * 2 - 2)
                V_.scalar_tensor_tensor(out=rs[:, u], in0=r1[:, u], scalar=1.5, in1=r0[:, u],
                                        op0=ALU.add, op1=ALU.mult)
                v.drain().then_inc(rs_ready, 1)

            def norm(i):
                last = isinstance(i, int) and i == NT // 4 - 1
                for u in range(2):
                    for k in range(2):
                        t = i * 4 + (2 * u + k)
                        need(v, xn_copied, t - 1)
                        need(v, xT_done, t - 1)
                        V_.tensor_scalar(xnb[k].rearrange("p (q d) -> p q d", q=NQ),
                                         XN[:, :, bass.ds(t, 1), :].rearrange("p q o d -> p q (o d)"),
                                         mv[:, 2 * u + k, 0:1], rs[:, u, k:k + 1],
                                         ALU.subtract, ALU.mult).then_inc(xn_norm, 1)
                    if not last:
                        stats(i * 2 + (u + 2), u, i + 1)
                    if not (last and u == 1):
                        invert(i * 2 + (u + 1), (u + 1) % 2)
            stats(0, 0, 0)
            stats(1, 1, 0)
            invert(0, 0)
            looped(v, 0, NT // 4 - 1, norm)
            norm(NT // 4 - 1)

            v.wait_ge(xn_copied, NT)
            v.wait_ge(xT_done, NT)

            def carry(i):
                for k in range(4):
                    g, b = i * 4 + k, k % 2
                    pS = bank[2 + b][:, 0:P].rearrange("p (h t) -> p h t", h=2)
                    v.wait_ge(s1_done, g + 1)
                    V_.tensor_scalar(ST[:, b], pS[:, 0], col(C_E0), None, ALU.mult)
                    v.drain()
                    V_.scalar_tensor_tensor(out=ST[:, b], in0=pS[:, 1], scalar=col(C_E1), in1=ST[:, b],
                                            op0=ALU.mult, op1=ALU.add).then_inc(s_ext, 1)
                    v.drain()
                    for s in range(NB):
                        V_.tensor_tensor_scan(
                            SC[:, b, s, 1:TPB + 1], QP[:, 7, bass.ds(g, 1)].to_broadcast([P, TPB]),
                            ST[:, b, s * TPB:(s + 1) * TPB], 0.0, ALU.mult, ALU.add)
                    v.drain()
                    need(v, s2_done, g - 1)
                    V_.tensor_tensor(
                        rhs2[:, b].rearrange("p d (s t) -> p d s t", s=NB),
                        maskcq[:, bass.ds(g, 1), :].rearrange("p o d -> p (o d)").unsqueeze(2).unsqueeze(3)
                        .to_broadcast([P, GC, NB, TPB]),
                        SC[:, b, :, 0:TPB].unsqueeze(1).to_broadcast([P, GC, NB, TPB]), ALU.mult
                    ).then_inc(rhs2_ready, 1)
            looped(v, 0, 4, carry)

            v.wait_ge(gate_done, NT)
            bc = lambda a, n: a.unsqueeze(2).to_broadcast([P, NT, n])
            desc = col(C_DESC, NE).unsqueeze(1).to_broadcast([P, NT, NE])
            V_.tensor_tensor(LG, pLG, bgs[:, :].unsqueeze(1).to_broadcast([P, NT, NE]), ALU.add).then_inc(lg_read, 1)
            v.drain()

            def best(m, r):
                V_.tensor_reduce(ra[:, m], LG, AX.X, ALU.max)
                v.drain()
                V_.tensor_tensor(LQ, LG, bc(ra[:, m], NE), ALU.is_equal)
                v.drain()
                V_.tensor_tensor(LQ, LQ, desc, ALU.mult)
                v.drain()
                V_.tensor_reduce(ra[:, r], LQ, AX.X, ALU.max)
                v.drain()
                V_.tensor_tensor(LQ, desc, bc(ra[:, r], NE), ALU.is_equal)
                v.drain()
            best(0, 1)
            V_.scalar_tensor_tensor(out=LG, in0=LQ, scalar=-3.0e38, in1=LG, op0=ALU.mult, op1=ALU.add)
            v.drain()
            best(2, 5)
            V_.tensor_tensor(ra[:, 3], ra[:, 2], ra[:, 0], ALU.subtract).then_inc(m_ready, 1)
            v.drain()
            V_.tensor_tensor(ra[:, 6], ra[:, 1], ra[:, 5], ALU.max)
            V_.tensor_tensor(ra[:, 7], ra[:, 1], ra[:, 5], ALU.min)
            V_.tensor_tensor(ra[:, 2], ra[:, 1], ra[:, 5], ALU.is_gt)
            v.drain()
            V_.tensor_scalar(ra[:, 0], ra[:, 6], -1.0, 8.0, ALU.mult, ALU.add)
            V_.tensor_scalar(ra[:, 6], ra[:, 6], 1.0, 5.0, ALU.mult, ALU.add)
            V_.tensor_scalar(ra[:, 7], ra[:, 7], -1.0, 8.0, ALU.mult, ALU.add)
            v.drain()
            V_.tensor_tensor(ra[:, 6], ra[:, 6], ra[:, 0], ALU.mult)
            v.drain()
            V_.scalar_tensor_tensor(out=ra[:, 6], in0=ra[:, 6], scalar=0.5, in1=ra[:, 7], op0=ALU.mult, op1=ALU.add)
            v.drain()
            for u in range(2):
                v.wait_ge(ks_out[u], 16 * 9)
            V_.tensor_tensor(OH, col(C_PAIR, NPAIR).unsqueeze(1).to_broadcast([P, NT, NPAIR]),
                             bc(ra[:, 6], NPAIR), ALU.is_equal).then_inc(oh_ready, 1)
            v.wait_ge(e_ready, 1)
            V_.tensor_scalar(ra[:, 0], ra[:, 4], 1.0, None, ALU.add)
            V_.tensor_scalar(ra[:, 1], ra[:, 2], -1.0, 1.0, ALU.mult, ALU.add)
            v.drain()
            V_.reciprocal(ra[:, 5], ra[:, 0])
            v.drain()
            V_.tensor_tensor(ra[:, 4], ra[:, 4], ra[:, 5], ALU.mult)
            v.drain()
            for f, (k1, k2) in enumerate(((2, 1), (1, 2))):
                V_.tensor_tensor(ra[:, 0], ra[:, 5], ra[:, k1], ALU.mult)
                V_.tensor_tensor(ra[:, 3], ra[:, 4], ra[:, k2], ALU.mult)
                v.drain()
                V_.tensor_tensor(TOK[:, :, 2 + f], ra[:, 0], ra[:, 3], ALU.add)
                v.drain()

            v.wait_ge(s_tab, 16)
            for c in range(4):
                v.wait_ge(cnt_done, c + 1)
                V_.tensor_copy(CNT[:, :, 16 * c:16 * c + 16],
                               bank[7 - c % 2][:, 0:16 * NPAIR].rearrange("p (t r) -> p r t", r=NPAIR)
                               ).then_inc(cnt_ev, 1)
            v.drain()
            flat = lambda a: a.rearrange("p r t -> p (r t)")
            V_.tensor_tensor_scan(flat(SCAN), col(C_ONE).to_broadcast([P, NPAIR * NT]), flat(CNT[:, :, :]), 0.0,
                                  ALU.mult, ALU.add)
            v.drain()
            V_.tensor_tensor(flat(SCAN), flat(SCAN), flat(CNT[:, :, :]), ALU.subtract)
            v.drain()
            V_.tensor_tensor(pr28[:, 0].unsqueeze(2), SCAN[:, :, NT - 1:NT], CNT[:, :, NT - 1:NT], ALU.add)
            v.drain()
            V_.tensor_tensor(pr28[:, 0].unsqueeze(2), pr28[:, 0].unsqueeze(2), SCAN[:, :, 0:1], ALU.subtract)
            v.drain()
            V_.tensor_scalar(pr28[:, 0], pr28[:, 0], P - 1.0, None, ALU.add)
            v.drain()
            V_.tensor_copy(pr28[:, 1].bitcast(i32), pr28[:, 0])
            v.drain()
            V_.tensor_scalar(pr28[:, 1].bitcast(i32), pr28[:, 1].bitcast(i32), 7, 7,
                             ALU.arith_shift_right, ALU.arith_shift_left)
            v.drain()
            V_.tensor_copy(pr28[:, 0], pr28[:, 1].bitcast(i32))
            v.drain()
            V_.tensor_tensor_scan(pr28[:, 2], col(C_ONE).to_broadcast([P, NPAIR]), pr28[:, 0], 0.0, ALU.mult, ALU.add)
            v.drain()
            V_.tensor_tensor(pr28[:, 3], pr28[:, 2], pr28[:, 0], ALU.subtract)
            v.drain()
            V_.tensor_tensor(pr28[:, 3].unsqueeze(2), pr28[:, 3].unsqueeze(2), SCAN[:, :, 0:1], ALU.subtract)
            for f, c in enumerate((C_DA, C_DB)):
                V_.scalar_tensor_tensor(out=pr28[:, 4 + f], in0=pr28[:, 2], scalar=col(C_IOTA), in1=col(c, NPAIR),
                                        op0=ALU.is_le, op1=ALU.mult)
            v.drain()
            for f in range(2):
                V_.tensor_reduce(AB[:, f:f + 1], pr28[:, 4 + f], AX.X, ALU.add)
            v.drain()
            V_.tensor_scalar(AB[:, 1:2], AB[:, 1:2], 1.0, None, ALU.add)
            V_.tensor_tensor(SCAN, SCAN, pr28[:, 3].unsqueeze(2).to_broadcast([P, NPAIR, NT]), ALU.add)
            v.drain().then_inc(ab_ready, 1)
            for c in range(4):
                v.wait_ge(pre_done, c + 1)
                V_.tensor_tensor(TMP, bank[7 - c % 2][:, 0:16 * NPAIR].rearrange("p (t r) -> p t r", r=NPAIR),
                                 SCAN[:, :, 16 * c:16 * c + 16].rearrange("p r t -> p t r"), ALU.add
                                 ).then_inc(pre_ev, 1)
                v.drain()
                V_.tensor_tensor(TMP, TMP, OH[:, 16 * c:16 * c + 16], ALU.mult)
                v.drain()
                V_.tensor_reduce(SLF[:, 16 * c:16 * c + 16], TMP, AX.X, ALU.add)
                v.drain()
            V_.tensor_copy(SLOT[:], SLF[:])
            v.drain().then_inc(slot_ready, 1)
            v.wait_ge(eo_done, 1)
            V_.tensor_copy(EO[:], bank[6][0:1, 0:2 * P]).then_inc(eo_ready, 1)

            looped(v, 4, NG // 4, carry, peel=0)

            v.wait_ge(s_tab, 32)
            v.wait_ge(s_be, 16)
            v.wait_ge(g_ix, 1)

            def norm3(b, n, i):
                v.wait_ge(gx[b], i * 16 + 16)
                need(v, x3_done, n - 1)
                V_.tensor_scalar(xm[b % 2], xg[b], TB[:, bass.ds(n, 1), 4], TB[:, bass.ds(n, 1), 5],
                                 ALU.subtract, ALU.mult).then_inc(xm_ready, 1)

            def final(b, n, i):
                v.wait_ge(gs[b], i * 16 + 16)
                v.wait_ge(g_ready, n + 1)
                need(v, o_out[b], i * 16)
                V_.tensor_tensor(gg[b % 2], gg[b % 2], sg[b], ALU.mult)
                v.drain()
                V_.tensor_tensor(og[b], gg[b % 2], xg[b], ALU.add).then_inc(o_ready, 1)

            def combine(b, n):
                wa, wb = TB[:, bass.ds(n, 1), 2], TB[:, bass.ds(n, 1), 3]
                ea = v.value_load(EO[0:1, bass.ds(n, 1)], min_val=0, max_val=NE - 1)
                eb = v.value_load(EO[0:1, bass.ds(n + P, 1)], min_val=0, max_val=NE - 1)
                row = lambda e: BE[:, bass.ds(e, 1), :].rearrange("p o h -> p (o h)")
                V_.tensor_scalar(uu[b], row(ea), wa, None, ALU.mult)
                v.drain()
                V_.scalar_tensor_tensor(out=uu[b], in0=row(eb), scalar=wb, in1=uu[b], op0=ALU.mult, op1=ALU.add)
                v.drain()
                v.wait_ge(mm_done, n + 1)
                V_.scalar_tensor_tensor(out=uu[b], in0=bank[2 + b][:, :], scalar=wa, in1=uu[b],
                                        op0=ALU.mult, op1=ALU.add)
                v.drain()
                need(v, g_ready, n - 1)
                V_.scalar_tensor_tensor(out=tt[b], in0=bank[4 + b][:, :], scalar=wb, in1=uu[b],
                                        op0=ALU.mult, op1=ALU.add).then_inc(t_ready, 1)

            norm3(0, 0, 0)
            norm3(1, 1, 0)

            def steps(i):
                for k in range(4):
                    n = i * 4 + k
                    if not (isinstance(n, int) and n + 2 >= NX):
                        norm3((k + 2) % 4, n + 2, i + (k + 2) // 4)
                    if not (isinstance(n, int) and n == 0):
                        final((k - 1) % 4, n - 1, i if k > 0 else i - 1)
                    combine(k % 2, n)
            looped(v, 0, NX // 4 - 1, steps, peel=2)
            steps(NX // 4 - 1)
            final(3, NX - 1, NX // 4 - 1)

        @block.tensor
        def _(pe):
            ident = col(C_ID, P)
            pe.wait_ge(s_const, 16 * 9)
            pe.wait_ge(s_taps, 1)

            def taps(i):
                for u in range(2):
                    j = i * 2 + u
                    pe.wait_ge(cm_ready, j + 1)
                    need(pe, ks_ev, j - 1)
                    for k in range(4):
                        last = nc.tensor.matmul(bank[2 + u][0:GC, k * P:(k + 1) * P], cmg[:, u, k],
                                                R[:, bass.ds(j * 4 + k, 1), :].rearrange("p o j -> p (o j)"),
                                                start=True, stop=True)
                    last.then_inc(pk_done, 1)
            looped(pe, 0, 8, taps)

            def turn(t, b):
                pe.wait_ge(xn_norm, t + 1)
                need(pe, xT_ev, t - 1)
                for c in range(NQ):
                    last = nc.tensor.transpose(bank[b][:, c * P:(c + 1) * P], xnb[b][:, c * P:(c + 1) * P], ident)
                last.then_inc(xT_done, 1)

            def gate(t, b):
                pe.wait_ge(xT_ev, t + 1)
                for c in range(NQ):
                    last = nc.tensor.matmul(bank[6][:, bass.ds(t * NE, NE)], xnT[b][:, c * P:(c + 1) * P], wg[:, c],
                                            start=(c == 0), stop=(c == NQ - 1))
                last.then_inc(gate_done, 1)

            def norm(i):
                for k in range(4):
                    turn(i * 4 + k, k % 2)
                    if k > 0:
                        gate(i * 4 + (k - 1), (k - 1) % 2)
                gate(i * 4 + 3, 1)
            looped(pe, 0, NT // 4, norm)

            def v_turn(g, k):
                pe.wait_ge(rg_ready, g + 1)
                need(pe, v_ev, g - 1)
                nc.tensor.transpose(bank[k % 2][:, 0:P], Rg[:, k], ident).then_inc(vt_done, 1)

            def states(g, k):
                pe.wait_ge(xg_ready, g + 1)
                pe.wait_ge(v_ev, g + 1)
                need(pe, s_ext, g - 1)
                for h in range(4):
                    last = nc.tensor.matmul(bank[2 + k % 2][32 * h:32 * h + 32, 0:P], V[:, k % 2, 32 * h:32 * h + 32],
                                            Xg[:, k % 2, 2 * h:2 * h + 2].rearrange("p d t -> p (d t)"),
                                            start=True, stop=True)
                last.then_inc(s1_done, 1)

            def within(g, k, i):
                pe.wait_ge(t_in[k % 2], i * 32 + 16 * (k // 2 + 1))
                need(pe, o_ev, g - 1)
                for c in range(GC):
                    last = nc.tensor.matmul(bank[4 + k % 2][:, c * NT:(c + 1) * NT], Tb[:, k % 2, c], Xg[:, k % 2, c],
                                            start=(c == 0), stop=False)
                last.then_inc(t_done, 1)

            def before(g, k):
                pe.wait_ge(rhs2_ready, g + 1)
                nc.tensor.matmul(bank[4 + k % 2][:, :], Rg[:, k], rhs2[:, k % 2].rearrange("p d t -> p (d t)"),
                                 start=False, stop=True).then_inc(s2_done, 1)

            def conv(i):
                for k in range(4):
                    g = i * 4 + k
                    more = not (isinstance(g, int) and g == NG - 1)
                    if more:
                        v_turn(g + 1, (k + 1) % 4)
                    within(g, k, i)
                    if more:
                        states(g + 1, (k + 1) % 4)
                    before(g, k)

            v_turn(0, 0)
            states(0, 0)
            looped(pe, 0, 4, conv)
            pe.wait_ge(oh_ready, 1)
            oh = OH.rearrange("p t r -> p (t r)")
            for c in range(8):
                if c < 4:
                    need(pe, cnt_ev, c - 1)
                else:
                    pe.wait_ge(cnt_ev, min(c - 1, 4))
                    need(pe, pre_ev, c - 5)
                nc.tensor.matmul(bank[7 - c % 2][:, 0:16 * NPAIR], (ones16 if c < 4 else tri16)[:],
                                 oh[:, (c % 4) * 16 * NPAIR:(c % 4 + 1) * 16 * NPAIR],
                                 start=True, stop=True).then_inc(cnt_done if c < 4 else pre_done, 1)
            pe.wait_ge(ab_ready, 1)
            pe.wait_ge(pre_ev, 4)
            for f in range(2):
                last = nc.tensor.matmul(bank[6][0:1, f * P:(f + 1) * P], AB[:, f:f + 1], ident, start=True, stop=True)
            last.then_inc(eo_done, 1)
            looped(pe, 4, NG // 4 - 1, conv, peel=0)
            conv(NG // 4 - 1)

            def turn3(n, b):
                pe.wait_ge(xm_ready, n + 1)
                need(pe, x3_ev, n - 1)
                for c in range(NQ):
                    last = nc.tensor.transpose(bank[b][:, c * P:(c + 1) * P], xm[b][:, c * P:(c + 1) * P], ident)
                last.then_inc(x3_done, 1)

            def products(n, b):
                ea = pe.value_load(EO[0:1, bass.ds(n, 1)], min_val=0, max_val=NE - 1)
                eb = pe.value_load(EO[0:1, bass.ds(n + P, 1)], min_val=0, max_val=NE - 1)
                pe.wait_ge(x3_ev, n + 1)
                need(pe, t_ready, n - 1)
                for c in range(NQ):
                    for y, e in ((2, ea), (4, eb)):
                        last = nc.tensor.matmul(bank[y + b][:, :], xmT[b][:, c * P:(c + 1) * P],
                                                W[:, c, bass.ds(e, 1), :].rearrange("p o h -> p (o h)"),
                                                start=(c == 0), stop=(c == NQ - 1))
                last.then_inc(mm_done, 1)

            pe.wait_ge(s_w, 16)
            pe.wait_ge(eo_ready, 1)
            turn3(0, 0)

            def steps(i):
                for k in range(4):
                    n = i * 4 + k
                    if not (isinstance(n, int) and n == NX - 1):
                        turn3(n + 1, (k + 1) % 2)
                    products(n, k % 2)
            looped(pe, 0, NX // 4 - 1, steps)
            steps(NX // 4 - 1)


def constants():
    import numpy as np
    c = np.zeros((P, NCST), np.float32)
    p = np.arange(P)
    c[:, C_ID:C_ID + P] = np.eye(P)
    c[:, C_TRI:C_TRI + P] = p[:, None] < p[None, :]
    c[:, C_MASK:C_MASK + GC] = p[:, None] // NS == np.arange(GC)
    c[:, C_DESC:C_DESC + NE] = NE - np.arange(NE)
    pairs = [(a, b) for a in range(NE) for b in range(a + 1, NE)]
    c[:, C_PAIR:C_PAIR + NPAIR] = 1 + np.arange(NPAIR)
    for k, at in ((0, C_DA), (1, C_DB)):
        c[:, at:at + NPAIR - 1] = np.diff([pair[k] for pair in pairs])
    c[:, C_ONE] = 1
    c[:, C_E0] = p // NS % 2 == 0
    c[:, C_E1] = p // NS % 2 == 1
    c[:, C_IOTA] = p * P
    tok = np.zeros((P, NT, TF), np.int32)
    tok[:, :, 0] = np.arange(NT) * P + p[:, None]
    tok[:, :, 1] = np.arange(NT) * P + (P - 1 - p[:, None])
    return c, tok


def kernel(L0_attn_x, L0_attn_delta, L0_attn_alpha, L0_attn_beta, L0_attn_gamma, L0_attn_omega,
           L0_ffn_We, L0_ffn_be, L0_ffn_Wg, L0_ffn_bg):
    import numpy as np
    import concourse.bacc as bacc
    from concourse.bass_utils import run_bass_kernel_spmd as run

    states = lambda a: np.ascontiguousarray(np.asarray(a).reshape(NG, P).T)
    cst, tok = constants()
    arrays = {
        "x": np.ascontiguousarray(L0_attn_x),
        "delta": states(L0_attn_delta), "alpha": states(L0_attn_alpha),
        "beta": states(L0_attn_beta), "gamma": states(L0_attn_gamma),
        "omega": np.ascontiguousarray(np.asarray(L0_attn_omega).reshape(NG, GC).T),
        "weT": np.ascontiguousarray(np.asarray(L0_ffn_We).reshape(NE, D, NQ, P).transpose(3, 2, 0, 1)),
        "be": np.ascontiguousarray(L0_ffn_be),
        "wgT": np.ascontiguousarray(np.asarray(L0_ffn_Wg).reshape(NE, NQ, P).transpose(2, 1, 0)),
        "bg": np.ascontiguousarray(L0_ffn_bg),
        "cst": cst, "tok": tok,
    }
    nc = bacc.Bacc("TRN2", target_bir_lowering=False, num_devices=1)
    args = [nc.dram_tensor(f"in_{n}", a.shape, mybir.dt.from_np(a.dtype), kind="ExternalInput").ap()
            for n, a in arrays.items()]
    out = nc.dram_tensor("out", L0_attn_x.shape, mybir.dt.float32, kind="ExternalOutput").ap()
    program(nc, *args, out)
    r = run(nc, [{f"in_{n}": a for n, a in arrays.items()}], core_ids=[0])
    return r.results[0]["out"]
```

```python
import concourse.bass as bass
from concourse import mybir
from contextlib import ExitStack

P = 128
D = 512
NB = 2
NT = 64
TPB = NT // NB
NS = 16
GC = P // NS
NG = D // GC
NQ = 4
GPQ = NG // NQ
NE = 8
NPAIR = NE * (NE - 1) // 2
NX = NT + NPAIR
TF = 8
EPS = 1e-5

C_ID, C_TRI, C_MASK, C_DESC, C_PAIR, C_DA, C_DB, C_ONE, C_E0, C_E1, C_IOTA = (
    0, 128, 256, 264, 272, 300, 328, 356, 357, 358, 359)
NCST = 360


def program(nc, x, delta, alpha, beta, gamma, omega, weT, be, wgT, bg, cst, tok, out):
    f32, i32, bf16 = mybir.dt.float32, mybir.dt.int32, mybir.dt.bfloat16
    ALU, ACT, AX = mybir.AluOpType, mybir.ActivationFunctionType, mybir.AxisListType
    with ExitStack() as ctx:
        def sb(name, shape, dt=f32):
            return ctx.enter_context(nc.sbuf_tensor(name, shape, dt))

        def sem(name):
            return ctx.enter_context(nc.semaphore(name))

        kr = nc.dram_tensor("kr", [D, 2 * P], f32, kind="Internal").ap()
        s_dram = nc.dram_tensor("s_rows", [NT * P, D], f32, kind="Internal").ap()
        table = nc.dram_tensor("slot_table", [NX * P, TF], f32, kind="Internal").ap()
        x_rows = x.rearrange("b l d -> (b l) d")
        out_rows = out.rearrange("b l d -> (b l) d")

        XN = sb("XN", [P, NQ, NT, P])
        R = sb("R", [P, NG, P])
        Tb = sb("Tb", [P, 2, GC, P])
        Xg = sb("Xg", [P, 2, GC, NT])
        Rg = sb("Rg", [P, 4, P])
        V = sb("V", [P, 2, 2, P])
        rhs2 = sb("rhs2", [P, 2, GC, NT])
        SC = sb("SC", [P, 2, NB, TPB + 1])
        maskcq = sb("maskcq", [P, NG, GC])
        C = sb("C", [P, NCST])
        tri16 = sb("tri16", [P, P], bf16)
        ones16 = sb("ones16", [P, P], bf16)
        wg = sb("wg", [P, NQ, NE])
        bgs = sb("bgs", [P, NE])
        om8 = sb("om8", [GC, NG])
        small = sb("small", [P, 14, NG])
        PW, SG, QP = small[:, 0:4], small[:, 4:6], small[:, 6:14]
        SLF = small[:, 12]
        ra = small[:, 0:8]
        pr28 = small[:, 8:12].rearrange("p a b -> p (a b)")[:, 0:8 * NPAIR].rearrange("p (a r) -> p a r", r=NPAIR)
        RT = sb("RT", [P, NPAIR * NT])
        CNT = sb("CNT", [P, NPAIR, NT], bf16)
        RB = sb("RB", [P, 1344])
        TOK = sb("TOK", [P, NT, TF])
        SLOT = sb("SLOT", [P, NT], i32)
        AB = sb("AB", [P, 2])
        EO = sb("EO", [1, 2 * P], i32)
        bst = sb("bst", [P, 4, 6])
        mv = sb("mv", [P, 4, 2])
        ve, sd, r0, r1 = sb("ve", [P, 2, 2]), sb("sd", [P, 2, 2]), sb("r0", [P, 2, 2]), sb("r1", [P, 2, 2])
        rs = sb("rs", [P, 2, 2])
        carrier = sb("carrier", [1, 1])

        xnb = [rhs2[:, u].rearrange("p a b -> p (a b)") for u in range(2)]
        xnT = [RT[:, u * D:(u + 1) * D] for u in range(2)]
        cmask = RT[:, 2 * D:3 * D].rearrange("p (g d) -> p g d", d=GC)
        LG = RT[:, 0:D].rearrange("p (t e) -> p t e", e=NE)
        LQ = RT[:, D:2 * D].rearrange("p (t e) -> p t e", e=NE)
        LR = RT[:, 2 * D:3 * D].rearrange("p (t e) -> p t e", e=NE)
        SCAN = RT[:, :].rearrange("p (r t) -> p r t", t=NT)
        tab0 = CNT[:, :, :].rearrange("p r t -> p (r t)")[:, 0:2 * NX * TF].bitcast(f32)
        kS = [RB[0:GC, u * D:(u + 1) * D].rearrange("p (g j) -> p g j", g=4) for u in range(2)]
        cmg = RT[:, 3 * D:3 * D + 8 * GC].rearrange("p (u g d) -> p u g d", u=2, d=GC)
        OH = RB[:, 0:NPAIR * NT // 2].bitcast(bf16).rearrange("p (t r) -> p t r", r=NPAIR)
        TMP = RB[:, NPAIR * NT // 2:NPAIR * NT // 2 + NPAIR * 16].rearrange("p (t r) -> p t r", r=NPAIR)
        pay = RB[:, 0:8 * TF].rearrange("p (k f) -> p k f", f=TF)
        six = RB[:, 8 * TF:8 * TF + 8].bitcast(i32)
        gix = RB[:, 8 * TF + 8:8 * TF + 16].bitcast(i32).rearrange("p (b f) -> p b f", f=2)
        oix = RB[:, 8 * TF + 16:8 * TF + 20].bitcast(i32)

        W = XN[:, 0:2].rearrange("p q t d -> p (q t d)").rearrange("p (c e h) -> p c e h", c=NQ, e=NE)

        def lanes(memory, *counts):
            at = [memory[:, i * D:(i + 1) * D] for i in range(sum(counts))]
            return [at[sum(counts[:k]):sum(counts[:k + 1])] for k in range(len(counts))]
        early = XN[:, 2].rearrange("p t d -> p (t d)")
        BE = early[:, 0:NE * D].rearrange("p (e h) -> p e h", e=NE)
        xg, xm, xmT = lanes(early[:, NE * D:], 4, 2, 2)
        sg, og = lanes(R[:, :, :].rearrange("p g j -> p (g j)"), 4, 4)
        uu, gg = lanes(Tb[:, :, :, :].rearrange("p u c j -> p (u c j)"), 2, 2)
        tt, = lanes(Xg[:, :, :, :].rearrange("p u c t -> p (u c t)"), 2)
        TB = RT[:, 0:NX * TF].rearrange("p (i f) -> p i f", f=TF)

        bank = [ctx.enter_context(nc.psum_tensor(f"bank{i}", [P, D], f32)) for i in range(8)]
        pLG = bank[6][:, :].rearrange("p (t e) -> p t e", e=NE)

        s_const, s_be, s_tab, s_w = sem("s_const"), sem("s_be"), sem("s_tab"), sem("s_w")
        s_sig = sem("s_sig")
        s_taps = sem("s_taps")
        cm_ready, pk_done, ks_ev, ks_om = sem("cm_ready"), sem("pk_done"), sem("ks_ev"), sem("ks_om")
        ks_out = [sem("ks_out0"), sem("ks_out1")]
        x_in = [sem("x_in0"), sem("x_in1")]
        st_ready, sd_ready, xn_norm = sem("st_ready"), sem("sd_ready"), sem("xn_norm")
        xn_copied, xT_done, xT_ev, gate_done = sem("xn_copied"), sem("xT_done"), sem("xT_ev"), sem("gate_done")
        rg_ready, xg_ready, vt_done, v_ev = sem("rg_ready"), sem("xg_ready"), sem("vt_done"), sem("v_ev")
        s1_done, s_ext, rhs2_ready = sem("s1_done"), sem("s_ext"), sem("rhs2_ready")
        t_in = [sem("t_in0"), sem("t_in1")]
        t_done, s2_done, o_ev = sem("t_done"), sem("s2_done"), sem("o_ev")
        s_out = [sem(f"s_out{q}") for q in range(NQ)]
        lg_read, m_ready, e_ready, oh_ready = sem("lg_read"), sem("m_ready"), sem("e_ready"), sem("oh_ready")
        cnt_done, cnt_ev, pre_done, pre_ev = sem("cnt_done"), sem("cnt_ev"), sem("pre_done"), sem("pre_ev")
        slot_ready, ab_ready, eo_done, eo_ready = sem("slot_ready"), sem("ab_ready"), sem("eo_done"), sem("eo_ready")
        pay_ready, sc_done = sem("pay_ready"), sem("sc_done")
        xn_rows, g_ix, gx, gs = sem("xn_rows"), sem("g_ix"), [sem(f"gx{b}") for b in range(4)], [sem(f"gs{b}") for b in range(4)]
        o_ix, o_out = sem("o_ix"), [sem(f"o_out{b}") for b in range(4)]
        xm_ready, x3_done, x3_ev, mm_done = sem("xm_ready"), sem("x3_done"), sem("x3_ev"), sem("mm_done")
        t_ready, g_ready, o_ready = sem("t_ready"), sem("g_ready"), sem("o_ready")

        block = ctx.enter_context(nc.Block())

        def col(c, n=1):
            return C[:, c:c + n]

        def need(eng, semaphore, value):
            if not isinstance(value, int) or value > 0:
                eng.wait_ge(semaphore, value)

        def looped(eng, lo, hi, body, peel=1):
            for i in range(lo, lo + peel):
                body(i)
            if hi > lo + peel:
                with eng.Fori(lo + peel, hi) as i:
                    body(i)

        @block.sync
        def _(sp):
            sp.dma_start(C[:], cst).then_inc(s_const, 16)
            for k, a in enumerate((delta, alpha, beta, gamma)):
                sp.dma_start(PW[:, k, :], a).then_inc(s_const, 16)
            sp.dma_start(om8[:], omega).then_inc(s_const, 16)
            sp.dma_start(wg[:], wgT).then_inc(s_const, 16)
            sp.dma_start(bgs[:], bg.partition_broadcast(P)).then_inc(s_const, 16)
            sp.dma_start(TOK[:].bitcast(i32), tok).then_inc(s_const, 16)

            x_pairs = x_rows.rearrange("(t p) (q d) -> p q t d", p=P, q=NQ)

            for u in range(2):
                for q in range(NQ):
                    sp.dma_start(XN[:, q, 2 * u:2 * u + 2, :], x_pairs[:, q, 2 * u:2 * u + 2, :]).then_inc(x_in[u], 16)
            sp.wait_ge(s_taps, 1)
            for u in range(2):
                sp.dma_start(kr[u * 256:(u + 1) * 256, P:2 * P].rearrange("(a p) j -> p a j", p=P),
                             rhs2[:, 1, 0:4, :].rearrange("p a b -> p (a b)").rearrange("p (a j) -> p a j", a=2)
                             ).then_inc(ks_out[u], 16)
            sp.dma_start(table.rearrange("(p i) f -> p (i f)", p=P), tab0).then_inc(s_tab, 16)
            kr_g = kr.rearrange("(g d) j -> d g j", d=GC)
            with sp.Fori(0, 8) as i:
                for u in range(2):
                    sp.wait_ge(ks_om, i * 2 + (u + 1))
                    sp.dma_start(kr_g[:, bass.ds(i * 8 + 4 * u, 4), 0:P], kS[u]).then_inc(ks_out[u], 16)
            with sp.Fori(1, NT // 4) as i:
                for u in range(2):
                    sp.wait_ge(x_in[u], i * 64)
                    for q in range(NQ):
                        sp.dma_start(XN[:, q, bass.ds(i * 4 + 2 * u, 2), :],
                                     x_pairs[:, q, bass.ds(i * 4 + 2 * u, 2), :]).then_inc(x_in[u], 16)
            for u in range(2):
                sp.wait_ge(ks_out[u], 16 * 9)
            kr_t = bass.AP(kr.tensor, 0, [[1, P], [2 * P, D], [1, P]])

            def blocks(i):
                for r in range(2):
                    g = i * 2 + r
                    need(sp, t_done, g - 1)
                    sp.dma_start(Tb[:, r], kr_t[:, bass.ds(g * GC, GC), :]).then_inc(t_in[r], 16)

            s_view = s_dram.rearrange("(t p) d -> p t d", p=P)

            def store_s(q, j):
                sp.wait_ge(o_ev, GPQ * (q + 1))
                sp.dma_start(s_view[:, bass.ds(j * 8, 8), q * P:(q + 1) * P], XN[:, q, bass.ds(j * 8, 8), :]
                             ).then_inc(s_out[q], 16)

            looped(sp, 0, 8, blocks)
            for q in range(1, NQ):
                if q == 3:
                    sp.wait_ge(s_out[0], 16 * 8)
                    sp.wait_ge(s_out[1], 16 * 8)
                with sp.Fori(0, 8) as j:
                    blocks(j + 8 * q)
                    store_s(q - 1, j)
                    if q == 3:
                        sp.dma_start(W[:, :, bass.ds(j, 1), :], weT[:, :, bass.ds(j, 1), :]).then_inc(s_w, 16)
            sp.wait_ge(sc_done, 16 * NT)
            sp.dma_start(TB, table.rearrange("(p i) f -> p i f", p=P)).then_inc(s_tab, 16)
            sp.wait_ge(s_out[2], 16 * 8)
            sp.dma_start(BE, be.rearrange("e h -> (e h)").partition_broadcast(P).rearrange("p (e h) -> p e h", e=NE)
                         ).then_inc(s_be, 16)
            for j in range(8):
                store_s(3, j)

        @block.gpsimd
        def _(pool):
            G_ = nc.gpsimd
            G_.memset(tab0, 0.0)
            G_.memset(V[:], 0.0)
            G_.memset(SC[:], 0.0)
            G_.memset(rhs2[:, 1], 0.0)
            G_.memset(ones16[:], 1.0)
            G_.memset(R[:, :, P - 1:P], 1.0)
            pool.drain()
            G_.memset(tab0.rearrange("p (i f) -> p i f", f=TF)[:, :, 0:2].bitcast(i32), NT * P)
            pool.wait_ge(s_const, 16 * 9)
            pool.wait_ge(s_sig, 1)
            G_.tensor_copy(tri16[:], col(C_TRI, P))
            G_.tensor_tensor(PW[:, 0], SG[:, 0], SG[:, 1], ALU.mult)
            G_.tensor_tensor(PW[:, 1], SG[:, 0], PW[:, 2], ALU.mult)
            G_.tensor_scalar(PW[:, 3], PW[:, 3], NS ** -0.5, None, ALU.mult)
            pool.drain()
            G_.tensor_scalar(QP[:, 0], PW[:, 0], -1.0, 1.0, ALU.mult, ALU.add)
            G_.tensor_tensor(PW[:, 2], PW[:, 3], PW[:, 1], ALU.mult)
            pool.drain()
            G_.tensor_tensor(PW[:, 3], PW[:, 2], QP[:, 0], ALU.mult)
            for k in range(7):
                w = 1 << k
                G_.tensor_tensor(R[:, :, P - 2 * w:P - w], R[:, :, P - w:P],
                                 QP[:, k].unsqueeze(2).to_broadcast([P, NG, w]), ALU.mult)
                G_.tensor_tensor(QP[:, k + 1], QP[:, k], QP[:, k], ALU.mult)
                pool.drain()
            mask = col(C_MASK, GC).unsqueeze(1).to_broadcast([P, NG, GC])
            G_.tensor_tensor(cmask, mask, PW[:, 2].unsqueeze(2).to_broadcast([P, NG, GC]), ALU.mult)
            G_.tensor_tensor(maskcq[:], mask, PW[:, 3].unsqueeze(2).to_broadcast([P, NG, GC]), ALU.mult)
            pool.drain().then_inc(s_taps, 1)

            def cm(u, j):
                G_.tensor_copy(cmg[:, u], cmask[:, bass.ds(j * 4, 4), :]).then_inc(cm_ready, 1)
            cm(0, 0)
            cm(1, 1)

            def taps(i, last):
                for u in range(2):
                    pool.wait_ge(ks_ev, i * 2 + (u + 1))
                    G_.tensor_tensor(kS[u][:, :, P - 1:P], kS[u][:, :, P - 1:P],
                                     om8[:, bass.ds(i * 8 + 4 * u, 4)].unsqueeze(2), ALU.add).then_inc(ks_om, 1)
                    if not last:
                        cm(u, i * 2 + (2 + u))
            with pool.Fori(0, 7) as i:
                taps(i, False)
            taps(7, True)

            def then_dma():
                nc.gpsimd.tensor_tensor(carrier[:], C[0:1, 0:1], C[0:1, 0:1], ALU.add)

            def scatter(i):
                for k in range(8):
                    t = i * 8 + k
                    nc.gpsimd.tensor_copy(pay[:, k].bitcast(i32), TOK[:, bass.ds(t, 1), :].rearrange("p o f -> p (o f)").bitcast(i32))
                    nc.gpsimd.tensor_copy(six[:, k:k + 1], SLOT[:, bass.ds(t, 1)]).then_inc(pay_ready, 1)
                    pool.wait_ge(pay_ready, t + 1)
                    then_dma()
                    nc.gpsimd.indirect_dma_start(
                        out=table, out_offset=bass.IndirectOffsetOnAxis(ap=six[:, k:k + 1], axis=0),
                        in_=pay[:, k], in_offset=None).then_inc(sc_done, 16)

            pool.wait_ge(slot_ready, 1)
            pool.wait_ge(s_tab, 16)
            with pool.Fori(0, NT // 8) as i:
                scatter(i)
                pool.wait_ge(sc_done, i * 128 + 128)

            pool.wait_ge(s_out[2], 16 * 8)
            for b in range(4):
                G_.memset(xg[b], 0.0)
            pool.wait_ge(rg_ready, NG)
            for b in range(4):
                last = G_.memset(sg[b], 0.0)
            last.then_inc(g_ix, 1)
            pool.wait_ge(g_ix, 1)
            pool.wait_ge(s_tab, 32)

            def gather(b, n):
                nc.gpsimd.tensor_copy(gix[:, b], TB[:, bass.ds(n, 1), 0:2].bitcast(i32).rearrange("p o f -> p (o f)")
                                      ).then_inc(g_ix, 1)
                pool.wait_ge(g_ix, n + 2)
                then_dma()
                nc.gpsimd.indirect_dma_start(
                    out=xg[b], out_offset=None, in_=x_rows,
                    in_offset=bass.IndirectOffsetOnAxis(ap=gix[:, b, 0:1], axis=0),
                    bounds_check=NT * P - 1, oob_is_err=False).then_inc(gx[b], 16)
                if isinstance(n, int) and n == 0:
                    for q in range(NQ):
                        pool.wait_ge(s_out[q], 16 * 8)
                nc.gpsimd.indirect_dma_start(
                    out=sg[b], out_offset=None, in_=s_dram,
                    in_offset=bass.IndirectOffsetOnAxis(ap=gix[:, b, 1:2], axis=0),
                    bounds_check=NT * P - 1, oob_is_err=False).then_inc(gs[b], 16)

            def give(b, n):
                nc.gpsimd.tensor_copy(oix[:, b:b + 1], TB[:, bass.ds(n, 1), 0:1].bitcast(i32).rearrange("p o f -> p (o f)")
                                      ).then_inc(o_ix, 1)
                pool.wait_ge(o_ix, n + 1)
                pool.wait_ge(o_ready, n + 1)
                then_dma()
                nc.gpsimd.indirect_dma_start(
                    out=out_rows, out_offset=bass.IndirectOffsetOnAxis(ap=oix[:, b:b + 1], axis=0),
                    in_=og[b], in_offset=None,
                    bounds_check=NT * P - 1, oob_is_err=False).then_inc(o_out[b], 16)

            for n in range(3):
                gather(n, n)

            def steps(i):
                for k in range(4):
                    gather((k + 3) % 4, i * 4 + (k + 3))
                    give(k, i * 4 + k)
            looped(pool, 0, NX // 4 - 1, steps)
            for k in range(4):
                n = NX - 4 + k
                if n + 3 < NX:
                    gather((k + 3) % 4, n + 3)
                give(k, n)
            for b in range(4):
                pool.wait_ge(o_out[b], 16 * (NX // 4))

        @block.scalar
        def _(act):
            act.wait_ge(s_const, 16 * 9)
            nc.scalar.activation(SG, PW[:, 0:2], ACT.Sigmoid).then_inc(s_sig, 1)

            def taps(i):
                for u in range(2):
                    act.wait_ge(pk_done, i * 2 + (u + 1))
                    act.wait_ge(ks_out[u], i * 16 + 16)
                    nc.scalar.activation(kS[u], bank[2 + u][0:GC, :].rearrange("p (g j) -> p g j", g=4),
                                         ACT.Copy).then_inc(ks_ev, 1)
            looped(act, 0, 8, taps)

            def root(n, u):
                act.wait_ge(st_ready, n + 1)
                nc.scalar.activation(sd[:, u], ve[:, u], ACT.Sqrt).then_inc(sd_ready, 1)

            def xt(i):
                for k in range(4):
                    t = i * 4 + k
                    if k % 2 == 0 and not (isinstance(i, int) and i == NT // 4 - 1 and k == 2):
                        root(i * 2 + (k // 2 + 1), (k // 2 + 1) % 2)
                    act.wait_ge(xn_norm, t + 1)
                    nc.scalar.activation(XN[:, :, bass.ds(t, 1), :].rearrange("p q o d -> p q (o d)"),
                                         xnb[k % 2].rearrange("p (q d) -> p q d", q=NQ), ACT.Copy).then_inc(xn_copied, 1)
                    act.wait_ge(xT_done, t + 1)
                    need(act, gate_done, t - 1)
                    nc.scalar.activation(xnT[k % 2], bank[k % 2][:, :], ACT.Copy).then_inc(xT_ev, 1)
            root(0, 0)
            looped(act, 0, NT // 4 - 1, xt)
            xt(NT // 4 - 1)

            act.wait_ge(xn_copied, NT)

            def v_out(b, g):
                act.wait_ge(vt_done, g + 1)
                need(act, s1_done, g - 1)
                for o in range(2):
                    nc.scalar.activation(V[:, b, o].rearrange("p (h r) -> p h r", r=2 * NS)[:, :, o * NS:(o + 1) * NS],
                                         bank[b][:, 0:P].rearrange("p (h r) -> p h r", r=2 * NS)[:, :, o * NS:(o + 1) * NS],
                                         ACT.Copy).then_inc(v_ev, 1)

            def group_of(g):
                return XN[:, bass.ds(g // GPQ, 1), :, bass.ds(g % GPQ * GC, GC)].rearrange("p o t d -> p (o t) d")

            def power_copy(b, g):
                need(act, s2_done, g - 3)
                nc.scalar.activation(Rg[:, b], R[:, bass.ds(g, 1), :].rearrange("p o j -> p (o j)"), ACT.Copy
                                     ).then_inc(rg_ready, 1)

            def x_copy(b, g):
                need(act, t_done, g - 1)
                nc.scalar.activation(Xg[:, b], group_of(g).rearrange("p t d -> p d t"), ACT.Copy).then_inc(xg_ready, 1)

            def s_back(b, g):
                act.wait_ge(xn_copied, NT)
                act.wait_ge(s2_done, g + 1)
                nc.scalar.activation(group_of(g), bank[4 + b][:, :].rearrange("p (d t) -> p t d", d=GC),
                                     ACT.Copy).then_inc(o_ev, 1)

            for g in range(3):
                power_copy(g, g)
            for g in range(2):
                x_copy(g, g)
            v_out(0, 0)

            def conv(i):
                for k in range(4):
                    g = i * 4 + k
                    left = NG - 1 - g if isinstance(g, int) else NG
                    if left >= 1:
                        v_out((k + 1) % 2, g + 1)
                    if left >= 3:
                        power_copy((k + 3) % 4, g + 3)
                    if left >= 2:
                        x_copy(k % 2, g + 2)
                    s_back(k % 2, g)
            looped(act, 0, 2, conv)
            act.wait_ge(m_ready, 1)
            nc.scalar.activation(ra[:, 4, :], ra[:, 3, :], ACT.Exp).then_inc(e_ready, 1)
            looped(act, 2, NG // 4 - 1, conv, peel=0)
            conv(NG // 4 - 1)

            def xt3(b, n):
                act.wait_ge(x3_done, n + 1)
                need(act, mm_done, n - 1)
                nc.scalar.activation(xmT[b], bank[b][:, :], ACT.Copy).then_inc(x3_ev, 1)

            def silu(b, n):
                act.wait_ge(t_ready, n + 1)
                need(act, o_ready, n - 1)
                nc.scalar.activation(gg[b], tt[b], ACT.Silu).then_inc(g_ready, 1)

            xt3(0, 0)

            def steps(i):
                for k in range(4):
                    xt3((k + 1) % 2, i * 4 + (k + 1))
                    silu(k % 2, i * 4 + k)
            looped(act, 0, NX // 4 - 1, steps)
            for k in range(4):
                if k < 3:
                    xt3((k + 1) % 2, NX - 4 + k + 1)
                silu(k % 2, NX - 4 + k)

        @block.vector
        def _(v):
            V_ = nc.vector
            v.wait_ge(s_const, 16 * 9)

            def stats(n, u, i):
                v.wait_ge(x_in[u], i * 64 + 64)
                for k in range(2):
                    V_.bn_stats(bst[:, 2 * u + k],
                                XN[:, :, bass.ds(n * 2 + k, 1), :].rearrange("p q o d -> p q (o d)"))
                v.drain()
                for k in range(2):
                    V_.bn_aggr(mv[:, 2 * u + k], bst[:, 2 * u + k])
                v.drain()
                V_.tensor_scalar(ve[:, u], mv[:, 2 * u:2 * u + 2, 1], EPS, None, ALU.add).then_inc(st_ready, 1)

            def invert(n, u):
                v.wait_ge(sd_ready, n + 1)
                V_.reciprocal(r0[:, u], sd[:, u])
                v.drain()
                V_.tensor_tensor(r1[:, u], r0[:, u], r0[:, u], ALU.mult)
                v.drain()
                V_.scalar_tensor_tensor(out=r1[:, u], in0=r1[:, u], scalar=-0.5, in1=ve[:, u],
                                        op0=ALU.mult, op1=ALU.mult)
                v.drain()
                V_.scalar_tensor_tensor(out=rs[:, u], in0=r1[:, u], scalar=1.5, in1=r0[:, u],
                                        op0=ALU.add, op1=ALU.mult)
                v.drain()
                V_.tensor_copy(TOK[:, bass.ds(n * 2, 2), 4], mv[:, 2 * u:2 * u + 2, 0])
                V_.tensor_copy(TOK[:, bass.ds(n * 2, 2), 5], rs[:, u])

            def norm(i):
                last = isinstance(i, int) and i == NT // 4 - 1
                for u in range(2):
                    for k in range(2):
                        t = i * 4 + (2 * u + k)
                        need(v, xn_copied, t - 1)
                        need(v, xT_done, t - 1)
                        V_.tensor_scalar(xnb[k].rearrange("p (q d) -> p q d", q=NQ),
                                         XN[:, :, bass.ds(t, 1), :].rearrange("p q o d -> p q (o d)"),
                                         mv[:, 2 * u + k, 0:1], rs[:, u, k:k + 1],
                                         ALU.subtract, ALU.mult).then_inc(xn_norm, 1)
                    if not last:
                        stats(i * 2 + (u + 2), u, i + 1)
                    if not (last and u == 1):
                        invert(i * 2 + (u + 1), (u + 1) % 2)
            stats(0, 0, 0)
            stats(1, 1, 0)
            invert(0, 0)
            looped(v, 0, NT // 4 - 1, norm)
            norm(NT // 4 - 1)

            v.wait_ge(xn_copied, NT)
            v.wait_ge(xT_done, NT)

            def carry(g, b):
                pS = bank[2 + b][:, 0:NT]
                v.wait_ge(s1_done, g + 1)
                for s in range(NB):
                    V_.tensor_tensor_scan(
                        SC[:, b, s, 1:TPB + 1], QP[:, 7, bass.ds(g, 1)].to_broadcast([P, TPB]),
                        pS[:, s * TPB:(s + 1) * TPB], 0.0, ALU.mult, ALU.add).then_inc(s_ext, 1)
                v.drain()
                need(v, s2_done, g - 1)
                V_.tensor_tensor(
                    rhs2[:, b].rearrange("p d (s t) -> p d s t", s=NB),
                    maskcq[:, bass.ds(g, 1), :].rearrange("p o d -> p (o d)").unsqueeze(2).unsqueeze(3)
                    .to_broadcast([P, GC, NB, TPB]),
                    SC[:, b, :, 0:TPB].unsqueeze(1).to_broadcast([P, GC, NB, TPB]), ALU.mult
                ).then_inc(rhs2_ready, 1)

            bc = lambda a, n: a.unsqueeze(2).to_broadcast([P, NT, n])
            desc = col(C_DESC, NE).unsqueeze(1).to_broadcast([P, NT, NE])
            flat = lambda a: a.rearrange("p r t -> p (r t)")
            counts, scan = flat(CNT[:, :, :]), flat(SCAN)
            HALF = NPAIR * NT // 2

            def logits():
                v.wait_ge(gate_done, NT)
                V_.tensor_tensor(LG, pLG, bgs[:, :].unsqueeze(1).to_broadcast([P, NT, NE]), ALU.add)
                v.drain()

            def greatest(m):
                V_.tensor_reduce(ra[:, m], LG, AX.X, ALU.max)
                v.drain()
                V_.tensor_tensor(LQ, LG, bc(ra[:, m], NE), ALU.is_equal)
                v.drain()

            def lowest(r):
                V_.tensor_tensor(LQ, LQ, desc, ALU.mult)
                v.drain()
                V_.tensor_reduce(ra[:, r], LQ, AX.X, ALU.max)
                v.drain()

            def without(r):
                V_.tensor_tensor(LQ, desc, bc(ra[:, r], NE), ALU.is_equal)
                v.drain()
                V_.scalar_tensor_tensor(out=LG, in0=LQ, scalar=-3.0e38, in1=LG, op0=ALU.mult, op1=ALU.add)
                v.drain()

            def pair_number():
                V_.tensor_tensor(ra[:, 3], ra[:, 2], ra[:, 0], ALU.subtract).then_inc(m_ready, 1)
                V_.tensor_tensor(ra[:, 6], ra[:, 1], ra[:, 5], ALU.max)
                V_.tensor_tensor(ra[:, 7], ra[:, 1], ra[:, 5], ALU.min)
                v.drain()
                V_.tensor_tensor(ra[:, 2], ra[:, 1], ra[:, 5], ALU.is_gt)
                V_.tensor_scalar(ra[:, 0], ra[:, 6], -1.0, 8.0, ALU.mult, ALU.add)
                v.drain()
                V_.tensor_scalar(ra[:, 6], ra[:, 6], 1.0, 5.0, ALU.mult, ALU.add)
                V_.tensor_scalar(ra[:, 7], ra[:, 7], -1.0, 8.0, ALU.mult, ALU.add)
                v.drain()
                V_.tensor_tensor(ra[:, 6], ra[:, 6], ra[:, 0], ALU.mult)
                v.drain()
                V_.scalar_tensor_tensor(out=ra[:, 6], in0=ra[:, 6], scalar=0.5, in1=ra[:, 7],
                                        op0=ALU.mult, op1=ALU.add)
                v.drain()

            def one_hot(h):
                for u in range(2):
                    v.wait_ge(ks_out[u], 16 * 9)
                t = slice(h * NT // 2, (h + 1) * NT // 2)
                V_.tensor_tensor(OH[:, t], col(C_PAIR, NPAIR).unsqueeze(1).to_broadcast([P, NT // 2, NPAIR]),
                                 ra[:, 6, t].unsqueeze(2).to_broadcast([P, NT // 2, NPAIR]), ALU.is_equal
                                 ).then_inc(oh_ready, 1)

            def weights():
                v.wait_ge(e_ready, 1)
                V_.tensor_scalar(ra[:, 0], ra[:, 4], 1.0, None, ALU.add)
                V_.tensor_scalar(ra[:, 1], ra[:, 2], -1.0, 1.0, ALU.mult, ALU.add)
                v.drain()
                V_.reciprocal(ra[:, 5], ra[:, 0])
                v.drain()
                V_.tensor_tensor(ra[:, 4], ra[:, 4], ra[:, 5], ALU.mult)
                v.drain()

            def weight(f):
                k1, k2 = ((2, 1), (1, 2))[f]
                V_.tensor_tensor(ra[:, 0], ra[:, 5], ra[:, k1], ALU.mult)
                V_.tensor_tensor(ra[:, 3], ra[:, 4], ra[:, k2], ALU.mult)
                v.drain()
                V_.tensor_tensor(TOK[:, :, 2 + f], ra[:, 0], ra[:, 3], ALU.add)
                v.drain()

            def count(c):
                v.wait_ge(s_tab, 16)
                v.wait_ge(cnt_done, c + 1)
                V_.tensor_copy(CNT[:, :, 16 * c:16 * c + 16],
                               bank[7 - c % 2][:, 0:16 * NPAIR].rearrange("p (t r) -> p r t", r=NPAIR)
                               ).then_inc(cnt_ev, 1)
                v.drain()

            def running(h):
                V_.tensor_tensor_scan(scan[:, h * HALF:(h + 1) * HALF], col(C_ONE).to_broadcast([P, HALF]),
                                      counts[:, h * HALF:(h + 1) * HALF],
                                      scan[:, HALF - 1:HALF] if h else 0.0, ALU.mult, ALU.add)
                v.drain()

            def before_tile():
                V_.tensor_tensor(scan, scan, counts, ALU.subtract)
                v.drain()

            def slots():
                V_.tensor_tensor(pr28[:, 0].unsqueeze(2), SCAN[:, :, NT - 1:NT], CNT[:, :, NT - 1:NT], ALU.add)
                v.drain()
                V_.scalar_tensor_tensor(out=pr28[:, 0].unsqueeze(2), in0=pr28[:, 0].unsqueeze(2), scalar=P - 1.0,
                                        in1=SCAN[:, :, 0:1], op0=ALU.add, op1=ALU.subtract)
                v.drain()
                V_.tensor_copy(pr28[:, 1].bitcast(i32), pr28[:, 0])
                v.drain()
                V_.tensor_scalar(pr28[:, 1].bitcast(i32), pr28[:, 1].bitcast(i32), 7, 7,
                                 ALU.arith_shift_right, ALU.arith_shift_left)
                v.drain()
                V_.tensor_copy(pr28[:, 0], pr28[:, 1].bitcast(i32))
                v.drain()

            def starts():
                V_.tensor_tensor_scan(pr28[:, 2], col(C_ONE).to_broadcast([P, NPAIR]), pr28[:, 0], 0.0,
                                      ALU.mult, ALU.add)
                v.drain()
                V_.tensor_tensor(pr28[:, 3], pr28[:, 2], pr28[:, 0], ALU.subtract)
                v.drain()
                V_.tensor_tensor(pr28[:, 3].unsqueeze(2), pr28[:, 3].unsqueeze(2), SCAN[:, :, 0:1], ALU.subtract)
                v.drain()

            def first_slot():
                V_.tensor_tensor(SCAN, SCAN, pr28[:, 3].unsqueeze(2).to_broadcast([P, NPAIR, NT]), ALU.add)
                v.drain()

            def experts():
                for f, c in enumerate((C_DA, C_DB)):
                    V_.scalar_tensor_tensor(out=pr28[:, 4 + f], in0=pr28[:, 2], scalar=col(C_IOTA), in1=col(c, NPAIR),
                                            op0=ALU.is_le, op1=ALU.mult)
                v.drain()
                for f in range(2):
                    V_.tensor_reduce(AB[:, f:f + 1], pr28[:, 4 + f], AX.X, ALU.add)
                v.drain()
                V_.tensor_scalar(AB[:, 1:2], AB[:, 1:2], 1.0, None, ALU.add)
                v.drain().then_inc(ab_ready, 1)

            def slot(c):
                v.wait_ge(pre_done, c + 1)
                V_.tensor_tensor(TMP, bank[7 - c % 2][:, 0:16 * NPAIR].rearrange("p (t r) -> p t r", r=NPAIR),
                                 SCAN[:, :, 16 * c:16 * c + 16].rearrange("p r t -> p t r"), ALU.add
                                 ).then_inc(pre_ev, 1)
                v.drain()
                V_.tensor_tensor(TMP, TMP, OH[:, 16 * c:16 * c + 16], ALU.mult)
                v.drain()
                V_.tensor_reduce(SLF[:, 16 * c:16 * c + 16], TMP, AX.X, ALU.add)
                v.drain()

            def table_rows():
                n, m = ra[:, 0].bitcast(i32), ra[:, 1].bitcast(i32)
                V_.tensor_copy(n, SLF)
                v.drain()
                V_.tensor_scalar(m, n, 7, None, ALU.arith_shift_right)
                V_.tensor_scalar(n, n, P - 1, None, ALU.bitwise_and)
                v.drain()
                V_.tensor_copy(ra[:, 2], n)
                V_.tensor_copy(ra[:, 3], m)
                v.drain()
                V_.scalar_tensor_tensor(out=ra[:, 4], in0=ra[:, 2], scalar=float(NX), in1=ra[:, 3],
                                        op0=ALU.mult, op1=ALU.add)
                v.drain()
                V_.tensor_copy(SLOT[:], ra[:, 4])
                v.drain().then_inc(slot_ready, 1)

            def tile_experts():
                v.wait_ge(eo_done, 1)
                V_.tensor_copy(EO[:], bank[6][0:1, 0:2 * P]).then_inc(eo_ready, 1)

            g = 0

            def then(part, *args):
                nonlocal g
                carry(g, g % 2)
                g += 1
                part(*args)

            then(logits)
            then(greatest, 0)
            then(lowest, 1)
            then(without, 1)
            then(greatest, 2)
            then(lowest, 5)
            then(pair_number)
            then(one_hot, 0)
            then(one_hot, 1)
            then(weights)
            then(weight, 0)
            then(weight, 1)
            for c in range(4):
                then(count, c)
            then(running, 0)
            then(running, 1)
            then(before_tile)
            then(slots)
            then(starts)
            then(first_slot)
            for c in range(4):
                then(slot, c)
            then(table_rows)
            then(experts)
            for k in range(4):
                carry(g + k, k % 2)
            tile_experts()
            with v.Fori(8, NG // 4) as i:
                for k in range(4):
                    carry(i * 4 + k, k % 2)

            v.wait_ge(s_tab, 32)

            def norm3(b, n, i):
                v.wait_ge(gx[b], i * 16 + 16)
                need(v, x3_done, n - 1)
                V_.tensor_scalar(xm[b % 2], xg[b], TB[:, bass.ds(n, 1), 4], TB[:, bass.ds(n, 1), 5],
                                 ALU.subtract, ALU.mult).then_inc(xm_ready, 1)

            def final(b, n, i):
                v.wait_ge(gs[b], i * 16 + 16)
                v.wait_ge(g_ready, n + 1)
                need(v, o_out[b], i * 16)
                V_.tensor_tensor(gg[b % 2], gg[b % 2], sg[b], ALU.mult)
                v.drain()
                V_.tensor_tensor(og[b], gg[b % 2], xg[b], ALU.add).then_inc(o_ready, 1)

            def combine(b, n):
                wa, wb = TB[:, bass.ds(n, 1), 2], TB[:, bass.ds(n, 1), 3]
                ea = v.value_load(EO[0:1, bass.ds(n, 1)], min_val=0, max_val=NE - 1)
                eb = v.value_load(EO[0:1, bass.ds(n + P, 1)], min_val=0, max_val=NE - 1)
                row = lambda e: BE[:, bass.ds(e, 1), :].rearrange("p o h -> p (o h)")
                V_.tensor_scalar(uu[b], row(ea), wa, None, ALU.mult)
                v.drain()
                V_.scalar_tensor_tensor(out=uu[b], in0=row(eb), scalar=wb, in1=uu[b], op0=ALU.mult, op1=ALU.add)
                v.drain()
                v.wait_ge(mm_done, n + 1)
                V_.scalar_tensor_tensor(out=uu[b], in0=bank[2 + b][:, :], scalar=wa, in1=uu[b],
                                        op0=ALU.mult, op1=ALU.add)
                v.drain()
                need(v, g_ready, n - 1)
                V_.scalar_tensor_tensor(out=tt[b], in0=bank[4 + b][:, :], scalar=wb, in1=uu[b],
                                        op0=ALU.mult, op1=ALU.add).then_inc(t_ready, 1)

            norm3(0, 0, 0)
            norm3(1, 1, 0)
            v.wait_ge(s_be, 16)
            v.wait_ge(o_ev, NG)

            def steps(i):
                for k in range(4):
                    n = i * 4 + k
                    if not (isinstance(n, int) and n + 2 >= NX):
                        norm3((k + 2) % 4, n + 2, i + (k + 2) // 4)
                    if not (isinstance(n, int) and n == 0):
                        final((k - 1) % 4, n - 1, i if k > 0 else i - 1)
                    combine(k % 2, n)
            looped(v, 0, NX // 4 - 1, steps, peel=2)
            steps(NX // 4 - 1)
            final(3, NX - 1, NX // 4 - 1)

        @block.tensor
        def _(pe):
            ident = col(C_ID, P)
            pe.wait_ge(s_const, 16 * 9)

            def taps(i):
                for u in range(2):
                    j = i * 2 + u
                    pe.wait_ge(cm_ready, j + 1)
                    need(pe, ks_ev, j - 1)
                    for k in range(4):
                        last = nc.tensor.matmul(bank[2 + u][0:GC, k * P:(k + 1) * P], cmg[:, u, k],
                                                R[:, bass.ds(j * 4 + k, 1), :].rearrange("p o j -> p (o j)"),
                                                start=True, stop=True)
                    last.then_inc(pk_done, 1)
            looped(pe, 0, 8, taps)

            def turn(t, b):
                pe.wait_ge(xn_norm, t + 1)
                need(pe, xT_ev, t - 1)
                for c in range(NQ):
                    last = nc.tensor.transpose(bank[b][:, c * P:(c + 1) * P], xnb[b][:, c * P:(c + 1) * P], ident)
                last.then_inc(xT_done, 1)

            def gate(t, b):
                pe.wait_ge(xT_ev, t + 1)
                for c in range(NQ):
                    last = nc.tensor.matmul(bank[6][:, bass.ds(t * NE, NE)], xnT[b][:, c * P:(c + 1) * P], wg[:, c],
                                            start=(c == 0), stop=(c == NQ - 1))
                last.then_inc(gate_done, 1)

            def norm(i):
                for k in range(4):
                    turn(i * 4 + k, k % 2)
                    if k > 0:
                        gate(i * 4 + (k - 1), (k - 1) % 2)
                gate(i * 4 + 3, 1)
            looped(pe, 0, NT // 4, norm)

            def v_turn(g, k):
                pe.wait_ge(rg_ready, g + 1)
                need(pe, v_ev, g * 2 - 2)
                nc.tensor.transpose(bank[k % 2][:, 0:P], Rg[:, k], ident).then_inc(vt_done, 1)

            def states(g, k):
                pe.wait_ge(xg_ready, g + 1)
                pe.wait_ge(v_ev, g * 2 + 2)
                need(pe, s_ext, g * 2 - 2)
                for h in range(4):
                    for o in range(2):
                        last = nc.tensor.matmul(bank[2 + k % 2][32 * h:32 * h + 32, 0:NT],
                                                V[:, k % 2, o, 32 * h:32 * h + 32], Xg[:, k % 2, 2 * h + o],
                                                start=(o == 0), stop=(o == 1))
                last.then_inc(s1_done, 1)

            def within(g, k, i):
                pe.wait_ge(t_in[k % 2], i * 32 + 16 * (k // 2 + 1))
                need(pe, o_ev, g - 1)
                for c in range(GC):
                    last = nc.tensor.matmul(bank[4 + k % 2][:, c * NT:(c + 1) * NT], Tb[:, k % 2, c], Xg[:, k % 2, c],
                                            start=(c == 0), stop=False)
                last.then_inc(t_done, 1)

            def before(g, k):
                pe.wait_ge(rhs2_ready, g + 1)
                nc.tensor.matmul(bank[4 + k % 2][:, :], Rg[:, k], rhs2[:, k % 2].rearrange("p d t -> p (d t)"),
                                 start=False, stop=True).then_inc(s2_done, 1)

            def conv(i):
                for k in range(4):
                    g = i * 4 + k
                    more = not (isinstance(g, int) and g == NG - 1)
                    if more:
                        v_turn(g + 1, (k + 1) % 4)
                    within(g, k, i)
                    if more:
                        states(g + 1, (k + 1) % 4)
                    before(g, k)
                    if isinstance(g, int):
                        after(g)

            oh = OH.rearrange("p t r -> p (t r)")

            def pairs(c, weights, done):
                nc.tensor.matmul(bank[7 - c % 2][:, 0:16 * NPAIR], weights[:],
                                 oh[:, c * 16 * NPAIR:(c + 1) * 16 * NPAIR], start=True, stop=True).then_inc(done, 1)

            def after(g):
                if 11 <= g < 15:
                    c = g - 11
                    pe.wait_ge(oh_ready, 2)
                    need(pe, cnt_ev, c - 1)
                    pairs(c, ones16, cnt_done)
                if 20 <= g < 24:
                    c = g - 20
                    pe.wait_ge(cnt_ev, 4)
                    need(pe, pre_ev, c - 1)
                    pairs(c, tri16, pre_done)
                if g == 29:
                    pe.wait_ge(ab_ready, 1)
                    pe.wait_ge(pre_ev, 4)
                    for f in range(2):
                        last = nc.tensor.matmul(bank[6][0:1, f * P:(f + 1) * P], AB[:, f:f + 1], ident,
                                                start=True, stop=True)
                    last.then_inc(eo_done, 1)

            v_turn(0, 0)
            states(0, 0)
            for i in range(8):
                conv(i)
            looped(pe, 8, NG // 4 - 1, conv, peel=0)
            conv(NG // 4 - 1)

            def turn3(n, b):
                pe.wait_ge(xm_ready, n + 1)
                need(pe, x3_ev, n - 1)
                for c in range(NQ):
                    last = nc.tensor.transpose(bank[b][:, c * P:(c + 1) * P], xm[b][:, c * P:(c + 1) * P], ident)
                last.then_inc(x3_done, 1)

            def products(n, b):
                ea = pe.value_load(EO[0:1, bass.ds(n, 1)], min_val=0, max_val=NE - 1)
                eb = pe.value_load(EO[0:1, bass.ds(n + P, 1)], min_val=0, max_val=NE - 1)
                pe.wait_ge(x3_ev, n + 1)
                need(pe, t_ready, n - 1)
                for c in range(NQ):
                    for y, e in ((2, ea), (4, eb)):
                        last = nc.tensor.matmul(bank[y + b][:, :], xmT[b][:, c * P:(c + 1) * P],
                                                W[:, c, bass.ds(e, 1), :].rearrange("p o h -> p (o h)"),
                                                start=(c == 0), stop=(c == NQ - 1))
                last.then_inc(mm_done, 1)

            pe.wait_ge(s_w, 16 * NE)
            pe.wait_ge(eo_ready, 1)
            turn3(0, 0)

            def steps(i):
                for k in range(4):
                    n = i * 4 + k
                    if not (isinstance(n, int) and n == NX - 1):
                        turn3(n + 1, (k + 1) % 2)
                    products(n, k % 2)
            looped(pe, 0, NX // 4 - 1, steps)
            steps(NX // 4 - 1)


def constants():
    import numpy as np
    c = np.zeros((P, NCST), np.float32)
    p = np.arange(P)
    c[:, C_ID:C_ID + P] = np.eye(P)
    c[:, C_TRI:C_TRI + P] = p[:, None] < p[None, :]
    c[:, C_MASK:C_MASK + GC] = p[:, None] // NS == np.arange(GC)
    c[:, C_DESC:C_DESC + NE] = NE - np.arange(NE)
    pairs = [(a, b) for a in range(NE) for b in range(a + 1, NE)]
    c[:, C_PAIR:C_PAIR + NPAIR] = 1 + np.arange(NPAIR)
    for k, at in ((0, C_DA), (1, C_DB)):
        c[:, at:at + NPAIR - 1] = np.diff([pair[k] for pair in pairs])
    c[:, C_ONE] = 1
    c[:, C_E0] = p // NS % 2 == 0
    c[:, C_E1] = p // NS % 2 == 1
    c[:, C_IOTA] = p * P
    tok = np.zeros((P, NT, TF), np.int32)
    tok[:, :, 0] = np.arange(NT) * P + p[:, None]
    tok[:, :, 1] = np.arange(NT) * P + (P - 1 - p[:, None])
    return c, tok


def kernel(L0_attn_x, L0_attn_delta, L0_attn_alpha, L0_attn_beta, L0_attn_gamma, L0_attn_omega,
           L0_ffn_We, L0_ffn_be, L0_ffn_Wg, L0_ffn_bg):
    import numpy as np
    import concourse.bacc as bacc
    from concourse.bass_utils import run_bass_kernel_spmd as run

    states = lambda a: np.ascontiguousarray(np.asarray(a).reshape(NG, P).T)
    cst, tok = constants()
    arrays = {
        "x": np.ascontiguousarray(L0_attn_x),
        "delta": states(L0_attn_delta), "alpha": states(L0_attn_alpha),
        "beta": states(L0_attn_beta), "gamma": states(L0_attn_gamma),
        "omega": np.ascontiguousarray(np.asarray(L0_attn_omega).reshape(NG, GC).T),
        "weT": np.ascontiguousarray(np.asarray(L0_ffn_We).reshape(NE, D, NQ, P).transpose(3, 2, 0, 1)),
        "be": np.ascontiguousarray(L0_ffn_be),
        "wgT": np.ascontiguousarray(np.asarray(L0_ffn_Wg).reshape(NE, NQ, P).transpose(2, 1, 0)),
        "bg": np.ascontiguousarray(L0_ffn_bg),
        "cst": cst, "tok": tok,
    }
    nc = bacc.Bacc("TRN2", target_bir_lowering=False, num_devices=1)
    args = [nc.dram_tensor(f"in_{n}", a.shape, mybir.dt.from_np(a.dtype), kind="ExternalInput").ap()
            for n, a in arrays.items()]
    out = nc.dram_tensor("out", L0_attn_x.shape, mybir.dt.float32, kind="ExternalOutput").ap()
    program(nc, *args, out)
    r = run(nc, [{f"in_{n}": a for n, a in arrays.items()}], core_ids=[0])
    return r.results[0]["out"]
```

```python
import concourse.bass as bass
from concourse import mybir
from contextlib import ExitStack

P = 128
D = 512
NB = 2
NT = 64
TPB = NT // NB
NS = 16
GC = P // NS
NG = D // GC
NQ = 4
GPQ = NG // NQ
NE = 8
NPAIR = NE * (NE - 1) // 2
MIN_ROUNDS = NT // 4
MAX_ROUNDS = -(-((NT * P + NPAIR * (P - 1)) // P) // 4)
NX = 4 * MAX_ROUNDS + 4
TF = 8
XS = 1024.0
TAPS_AT = 6
EPS = 1e-5

C_ID, C_TRI, C_MASK, C_DESC, C_PAIR, C_DA, C_DB, C_ONE, C_E0, C_E1, C_IOTA = (
    0, 128, 256, 264, 272, 300, 328, 356, 357, 358, 359)
NCST = 360


def program(nc, x, delta, alpha, beta, gamma, omega, weT, be, wgT, bg, cst, tok, out):
    f32, i32, bf16, f16 = mybir.dt.float32, mybir.dt.int32, mybir.dt.bfloat16, mybir.dt.float16
    ALU, ACT, AX = mybir.AluOpType, mybir.ActivationFunctionType, mybir.AxisListType
    with ExitStack() as ctx:
        def sb(name, shape, dt=f32):
            return ctx.enter_context(nc.sbuf_tensor(name, shape, dt))

        def sem(name):
            return ctx.enter_context(nc.semaphore(name))

        kr = nc.dram_tensor("kr", [D, 2 * P], f32, kind="Internal").ap()
        s_dram = nc.dram_tensor("s_rows", [NT * P, D], f32, kind="Internal").ap()
        table = nc.dram_tensor("slot_table", [NX * P, TF], f32, kind="Internal").ap()
        x_rows = x.rearrange("b l d -> (b l) d")
        out_rows = out.rearrange("b l d -> (b l) d")

        XN = sb("XN", [P, NQ, NT, P])
        R = sb("R", [P, NG, P])
        Tb = sb("Tb", [P, 2, GC, P])
        Xg = sb("Xg", [P, 2, GC, NT])
        Rg = sb("Rg", [P, 4, P])
        V = sb("V", [P, 2, 2, P])
        rhs2 = sb("rhs2", [P, 2, GC, NT])
        SC = sb("SC", [P, 2, NB, TPB + 1])
        maskcq = sb("maskcq", [P, NG, GC])
        C = sb("C", [P, NCST])
        tri16 = sb("tri16", [P, P], bf16)
        ones16 = sb("ones16", [P, P], bf16)
        wg = sb("wg", [P, NQ, NE])
        bgs = sb("bgs", [P, NE])
        om8 = sb("om8", [GC, NG])
        wmax = sb("wmax", [P, 4 * NE])
        scl = sb("scl", [P, 4])
        small = sb("small", [P, 14, NG])
        PW, SG, QP = small[:, 0:4], small[:, 4:6], small[:, 6:14]
        SLF = small[:, 12]
        ra = small[:, 0:8]
        pr28 = small[:, 8:12].rearrange("p a b -> p (a b)")[:, 0:8 * NPAIR].rearrange("p (a r) -> p a r", r=NPAIR)
        RT = sb("RT", [P, NPAIR * NT])
        CNT = sb("CNT", [P, NPAIR, NT], bf16)
        RB = sb("RB", [P, 1344])
        TOK = sb("TOK", [P, NT, TF])
        SLOT = sb("SLOT", [P, NT], i32)
        AB = sb("AB", [P, 2])
        EO = sb("EO", [1, P], i32)
        bst = sb("bst", [P, 4, 6])
        mv = sb("mv", [P, 4, 2])
        ve, sd, r0, r1, rs = sb("ve", [P, 4]), sb("sd", [P, 4]), sb("r0", [P, 4]), sb("r1", [P, 4]), sb("rs", [P, 4])
        last_round = sb("last_round", [P, 1], i32)
        carrier = sb("carrier", [1, 1])

        xnb = [m[:, u].rearrange("p a b -> p (a b)") for u in range(2) for m in (rhs2, Xg)]
        xnT = [RT[:, u * D:(u + 1) * D] for u in range(2)]
        cmask = RT[:, 2 * D:3 * D].rearrange("p (g d) -> p g d", d=GC)
        LG = RT[:, 0:D].rearrange("p (t e) -> p t e", e=NE)
        LQ = RT[:, D:2 * D].rearrange("p (t e) -> p t e", e=NE)
        SCAN = RT[:, :].rearrange("p (r t) -> p r t", t=NT)
        tab0 = CNT[:, :, :].rearrange("p r t -> p (r t)")[:, 0:2 * NX * TF].bitcast(f32)
        kS = [RB[0:GC, u * D:(u + 1) * D].rearrange("p (g j) -> p g j", g=4) for u in range(2)]
        cmg = RT[:, 3 * D:3 * D + 8 * GC].rearrange("p (u g d) -> p u g d", u=2, d=GC)
        OH = RB[:, 0:NPAIR * NT // 2].bitcast(bf16).rearrange("p (t r) -> p t r", r=NPAIR)
        TMP = RB[:, NPAIR * NT // 2:NPAIR * NT // 2 + NPAIR * 16].rearrange("p (t r) -> p t r", r=NPAIR)
        pay = RB[:, 0:8 * TF].rearrange("p (k f) -> p k f", f=TF)
        six = RB[:, 8 * TF:8 * TF + 8].bitcast(i32)
        gix = RB[:, 8 * TF + 8:8 * TF + 16].bitcast(i32).rearrange("p (b f) -> p b f", f=2)
        oix = RB[:, 8 * TF + 16:8 * TF + 20].bitcast(i32)

        CNTf = CNT[:, :, :].rearrange("p r t -> p (r t)").bitcast(f32)
        lgS = [CNTf[0:NE, D:D + 2 * P], RB[0:NE, 2 * D:2 * D + 2 * P]]

        W16 = XN[:, 0:2].rearrange("p q t d -> p (q t d)").bitcast(f16).rearrange(
            "p (e f c h) -> p e f c h", e=NE, f=2, c=NQ)

        def lanes(memory, *counts):
            at = [memory[:, i * D:(i + 1) * D] for i in range(sum(counts))]
            return [at[sum(counts[:k]):sum(counts[:k + 1])] for k in range(len(counts))]
        early = XN[:, 2].rearrange("p t d -> p (t d)")
        BE = early[:, 0:NE * D].rearrange("p (e h) -> p e h", e=NE)
        xg, xm, xmT = lanes(early[:, NE * D:], 4, 2, 2)
        xmT = [m.bitcast(f16).rearrange("p (f k) -> p f k", f=2) for m in xmT]
        sg, og = lanes(R[:, NG // 2:].rearrange("p g j -> p (g j)"), 4, 4)
        wch = [Rg[:, :, :].rearrange("p k j -> p (k j)"), CNTf[:, 0:D]]
        stage = R[:, 0:NQ * D // P].rearrange("p g j -> p (g j)").rearrange("p (c h) -> p c h", c=NQ)
        spread = RT[:, 3 * D + 64:3 * D + 64 + P]
        ba, bb = lanes(Tb[:, :, :, :].rearrange("p u c j -> p (u c j)"), 2, 2)
        tt, = lanes(Xg[:, :, :, :].rearrange("p u c t -> p (u c t)"), 2)
        gg, = lanes(rhs2[:, :, :, :].rearrange("p u c t -> p (u c t)"), 2)
        TB = RT[:, 0:NX * TF].rearrange("p (i f) -> p i f", f=TF)

        bank = [ctx.enter_context(nc.psum_tensor(f"bank{i}", [P, D], f32)) for i in range(8)]
        pLG = bank[6][:, :].rearrange("p (t e) -> p t e", e=NE)

        s_par = sem("s_par")
        s_tok, s_const, s_be, s_tab = sem("s_tok"), sem("s_const"), sem("s_be"), sem("s_tab")
        sc_zero = sem("sc_zero")
        tk_ready = sem("tk_ready")
        kz_out = sem("kz_out")
        lg_ev, lg_done = sem("lg_ev"), sem("lg_done")
        w_in, w_free = [sem("w_in0"), sem("w_in1")], sem("w_free")
        wm_ready, wm_done, scl_ready = sem("wm_ready"), sem("wm_done"), sem("scl_ready")
        hi_ready, lo_ready, xhi_ready, xlo_ready = sem("hi_ready"), sem("lo_ready"), sem("xhi_ready"), sem("xlo_ready")
        st_in = [sem("st_in0"), sem("st_in1")]
        s_sig = sem("s_sig")
        z_ready = sem("z_ready")
        cm_ready, pk_done, ks_ev, ks_om = sem("cm_ready"), sem("pk_done"), sem("ks_ev"), sem("ks_om")
        ks_out = [sem("ks_out0"), sem("ks_out1")]
        x_in = [sem(f"x_in{k}") for k in range(4)]
        st_ready, sd_ready, xn_norm = sem("st_ready"), sem("sd_ready"), sem("xn_norm")
        xn_placed, xT_done, xT_ev, gate_done = sem("xn_placed"), sem("xT_done"), sem("xT_ev"), sem("gate_done")
        rg_ready, xg_ready, vt_done, v_ev = sem("rg_ready"), sem("xg_ready"), sem("vt_done"), sem("v_ev")
        s1_done, s_ext, rhs2_ready = sem("s1_done"), sem("s_ext"), sem("rhs2_ready")
        t_in = [sem("t_in0"), sem("t_in1")]
        t_done, s2_done, o_ev = sem("t_done"), sem("s2_done"), sem("o_ev")
        s_out = [sem(f"s_out{q}") for q in range(NQ)]
        m_ready, e_ready, oh_ready = sem("m_ready"), sem("e_ready"), sem("oh_ready")
        cnt_done, cnt_ev, pre_done, pre_ev = sem("cnt_done"), sem("cnt_ev"), sem("pre_done"), sem("pre_ev")
        slot_ready, ab_ready, eo_done, eo_ready = sem("slot_ready"), sem("ab_ready"), sem("eo_done"), sem("eo_ready")
        pay_ready, sc_done = sem("pay_ready"), sem("sc_done")
        g_ix, gx, gs = sem("g_ix"), [sem(f"gx{b}") for b in range(4)], [sem(f"gs{b}") for b in range(4)]
        o_ix, o_out = sem("o_ix"), [sem(f"o_out{b}") for b in range(4)]
        xm_ready, x3_done, mm_done = sem("xm_ready"), sem("x3_done"), sem("mm_done")
        b_ready, b_used, t_half = sem("b_ready"), sem("b_used"), sem("t_half")
        t_ready, g_ready, o_ready = sem("t_ready"), sem("g_ready"), sem("o_ready")

        block = ctx.enter_context(nc.Block())

        def col(c, n=1):
            return C[:, c:c + n]

        def need(eng, semaphore, value):
            if not isinstance(value, int) or value > 0:
                eng.wait_ge(semaphore, value)

        def experts_of(eng, n):
            both = eng.value_load(EO[0:1, bass.ds(n, 1)], min_val=0, max_val=NE * NE - 1)
            return both // NE, both % NE

        def each_round(eng, body):
            last = eng.value_load(last_round[0:1, 0:1], min_val=MIN_ROUNDS - 1, max_val=MAX_ROUNDS - 1)
            looped(eng, 0, MIN_ROUNDS, body)
            with eng.Fori(MIN_ROUNDS, MAX_ROUNDS) as i:
                with eng.If(i <= last):
                    body(i)
            return last

        def looped(eng, lo, hi, body, peel=1):
            for i in range(lo, lo + peel):
                body(i)
            if hi > lo + peel:
                with eng.Fori(lo + peel, hi) as i:
                    body(i)

        @block.sync
        def _(sp):
            x_tiles = x_rows.rearrange("(t p) (q d) -> p t q d", p=P, q=NQ)

            def tiles(i):
                for k in range(4):
                    need(sp, x_in[k], i * 16)
                    sp.dma_start(XN[:, :, bass.ds(i * 4 + k, 1), :].rearrange("p q o d -> p q (o d)"),
                                 x_tiles[:, bass.ds(i * 4 + k, 1)].rearrange("p o q d -> p (o q) d")
                                 ).then_inc(x_in[k], 16)
            for k, a in enumerate((delta, alpha)):
                sp.dma_start(PW[:, k, :], a).then_inc(s_par, 16)
            tiles(0)
            sp.dma_start(TOK[:].bitcast(i32), tok).then_inc(s_tok, 16)
            tiles(1)
            sp.dma_start(C[:], cst).then_inc(s_const, 16)
            for k, a in ((2, beta), (3, gamma)):
                sp.dma_start(PW[:, k, :], a).then_inc(s_const, 16)
            sp.dma_start(om8[:], omega).then_inc(s_const, 16)
            sp.dma_start(wg[:], wgT).then_inc(s_const, 16)
            sp.dma_start(bgs[:], bg.partition_broadcast(P)).then_inc(s_const, 16)

            sp.wait_ge(z_ready, 1)
            for u in range(2):
                sp.dma_start(kr[u * 256:(u + 1) * 256, P:2 * P].rearrange("(a p) j -> p a j", p=P), V[:, 0]
                             ).then_inc(kz_out, 16)
            sp.dma_start(table.rearrange("(p i) f -> p (i f)", p=P), tab0).then_inc(s_tab, 16)

            we_rows = weT.rearrange("p c e h -> p (c e) h")

            sp.wait_ge(s_tab, 16)

            def chunks(i):
                for u in range(2):
                    need(sp, w_free, i * 2 + (u - 1))
                    sp.dma_start(wch[u].rearrange("p (o h) -> p o h", o=1), we_rows[:, bass.ds(i * 2 + u, 1), :]
                                 ).then_inc(w_in[u], 16)

            def load(i):
                chunks(i - 2)
                tiles(i)
            looped(sp, 2, NT // 4, load)
            chunks(NT // 4 - 2)
            chunks(NT // 4 - 1)
            sp.wait_ge(kz_out, 32)
            for u in range(2):
                sp.wait_ge(ks_out[u], 16 * 8)
            kr_t = bass.AP(kr.tensor, 0, [[1, P], [2 * P, D], [1, P]])

            def blocks(i):
                for r in range(2):
                    g = i * 2 + r
                    need(sp, t_done, g - 1)
                    sp.dma_start(Tb[:, r], kr_t[:, bass.ds(g * GC, GC), :]).then_inc(t_in[r], 16)

            s_view = s_dram.rearrange("(t p) d -> p t d", p=P)

            def store_s(q, j):
                sp.wait_ge(o_ev, GPQ * (q + 1))
                sp.dma_start(s_view[:, bass.ds(j * 8, 8), q * P:(q + 1) * P], XN[:, q, bass.ds(j * 8, 8), :]
                             ).then_inc(s_out[q], 16)

            looped(sp, 0, 8, blocks)
            def half_expert(e, r):
                need(sp, lo_ready, e * 4 + (2 * r - 2))
                sp.dma_start(stage[:, 2 * r:2 * r + 2], weT[:, 2 * r:2 * r + 2, bass.ds(e, 1), :]
                             .rearrange("p c o h -> p c (o h)")).then_inc(st_in[r], 16)

            def quarter(q, m, stored):
                for r in range(2):
                    blocks(m * 2 + (GPQ // 2 * q + r))
                    if q > 1 and not (isinstance(m, int) and q == 3 and m == 3 and r == 1):
                        half_expert(m + (4 * (q - 2) + r), 1 - r)
                    for j in stored[r]:
                        store_s(q - 1, j)
            looped(sp, 0, 4, lambda m: quarter(1, m, ([m * 2], [m * 2 + 1])), peel=0)
            half_expert(0, 0)
            looped(sp, 0, 4, lambda m: quarter(2, m, ([m * 2], [m * 2 + 1])))
            for m, stored in enumerate((([0, 1], [2, 3]), ([4, 5], [6, 7]), ([], []), ([], []))):
                quarter(3, m, stored)
                if m == 2:
                    sp.wait_ge(sc_done, 16 * NT)
                    sp.dma_start(TB, table.rearrange("(p i) f -> p i f", p=P)).then_inc(s_tab, 16)
            sp.wait_ge(s_out[2], 16 * 8)
            sp.dma_start(BE, be.rearrange("e h -> (e h)").partition_broadcast(P)
                         .rearrange("p (e h) -> p e h", e=NE)).then_inc(s_be, 16)
            for j in range(8):
                store_s(3, j)

        @block.gpsimd
        def _(pool):
            G_ = nc.gpsimd
            G_.memset(V[:], 0.0)
            G_.memset(tab0, 0.0)
            pool.drain()
            G_.memset(tab0.rearrange("p (i f) -> p i f", f=TF)[:, :, 0:2].bitcast(i32), NT * P).then_inc(z_ready, 1)
            G_.memset(R[:, :, P - 1:P], 1.0)
            pool.wait_ge(s_const, 16 * 6)
            pool.wait_ge(s_sig, 1)
            G_.tensor_copy(tri16[:], col(C_TRI, P))
            G_.tensor_tensor(PW[:, 0], SG[:, 0], SG[:, 1], ALU.mult)
            G_.tensor_tensor(PW[:, 1], SG[:, 0], PW[:, 2], ALU.mult)
            G_.tensor_scalar(PW[:, 3], PW[:, 3], NS ** -0.5, None, ALU.mult)
            pool.drain()
            G_.tensor_scalar(QP[:, 0], PW[:, 0], -1.0, 1.0, ALU.mult, ALU.add)
            G_.tensor_tensor(PW[:, 2], PW[:, 3], PW[:, 1], ALU.mult)
            pool.drain()
            G_.tensor_tensor(PW[:, 3], PW[:, 2], QP[:, 0], ALU.mult)
            for k in range(7):
                w = 1 << k
                G_.tensor_tensor(R[:, :, P - 2 * w:P - w], R[:, :, P - w:P],
                                 QP[:, k].unsqueeze(2).to_broadcast([P, NG, w]), ALU.mult)
                G_.tensor_tensor(QP[:, k + 1], QP[:, k], QP[:, k], ALU.mult)
                pool.drain()
            mask = col(C_MASK, GC).unsqueeze(1).to_broadcast([P, NG, GC])
            G_.tensor_tensor(cmask, mask, PW[:, 2].unsqueeze(2).to_broadcast([P, NG, GC]), ALU.mult)
            G_.tensor_tensor(maskcq[:], mask, PW[:, 3].unsqueeze(2).to_broadcast([P, NG, GC]), ALU.mult)
            pool.drain()

            def cm(u, j):
                G_.tensor_copy(cmg[:, u], cmask[:, bass.ds(j * 4, 4), :]).then_inc(cm_ready, 1)
            cm(0, 0)
            cm(1, 1)

            kr_g = kr.rearrange("(g d) j -> d g j", d=GC)

            def taps(i, last):
                for u in range(2):
                    pool.wait_ge(ks_ev, i * 2 + (u + 1))
                    G_.tensor_tensor(kS[u][:, :, P - 1:P], kS[u][:, :, P - 1:P],
                                     om8[:, bass.ds(i * 8 + 4 * u, 4)].unsqueeze(2), ALU.add).then_inc(ks_om, 1)
                    pool.wait_ge(ks_om, i * 2 + (u + 1))
                    G_.dma_start(kr_g[:, bass.ds(i * 8 + 4 * u, 4), 0:P], kS[u]).then_inc(ks_out[u], 16)
                    if not last:
                        cm(u, i * 2 + (2 + u))
            with pool.Fori(0, 7) as i:
                taps(i, False)
            taps(7, True)
            G_.memset(SC[:], 0.0)
            G_.memset(ones16[:], 1.0).then_inc(sc_zero, 1)

            def then_dma():
                nc.gpsimd.tensor_tensor(carrier[:], C[0:1, 0:1], C[0:1, 0:1], ALU.add)

            def scatter(i):
                for k in range(8):
                    t = i * 8 + k
                    nc.gpsimd.tensor_copy(pay[:, k].bitcast(i32),
                                          TOK[:, bass.ds(t, 1), :].rearrange("p o f -> p (o f)").bitcast(i32))
                    nc.gpsimd.tensor_copy(six[:, k:k + 1], SLOT[:, bass.ds(t, 1)]).then_inc(pay_ready, 1)
                    pool.wait_ge(pay_ready, t + 1)
                    then_dma()
                    nc.gpsimd.indirect_dma_start(
                        out=table, out_offset=bass.IndirectOffsetOnAxis(ap=six[:, k:k + 1], axis=0),
                        in_=pay[:, k], in_offset=None).then_inc(sc_done, 16)

            pool.wait_ge(slot_ready, 1)
            pool.wait_ge(s_tab, 16)
            with pool.Fori(0, NT // 8) as i:
                scatter(i)
                pool.wait_ge(sc_done, i * 128 + 128)

            pool.wait_ge(s_out[2], 16 * 8)
            for b in range(4):
                G_.memset(xg[b], 0.0)
            pool.wait_ge(rg_ready, NG)
            for b in range(4):
                last = G_.memset(sg[b], 0.0)
            last.then_inc(g_ix, 1)
            pool.wait_ge(g_ix, 1)
            pool.wait_ge(s_tab, 32)

            def gather_x(b, n):
                nc.gpsimd.tensor_copy(gix[:, b], TB[:, bass.ds(n, 1), 0:2].bitcast(i32).rearrange("p o f -> p (o f)")
                                      ).then_inc(g_ix, 1)
                pool.wait_ge(g_ix, n + 2)
                then_dma()
                nc.gpsimd.indirect_dma_start(
                    out=xg[b], out_offset=None, in_=x_rows,
                    in_offset=bass.IndirectOffsetOnAxis(ap=gix[:, b, 0:1], axis=0),
                    bounds_check=NT * P - 1, oob_is_err=False).then_inc(gx[b], 16)

            def gather_s(b, n):
                nc.gpsimd.indirect_dma_start(
                    out=sg[b], out_offset=None, in_=s_dram,
                    in_offset=bass.IndirectOffsetOnAxis(ap=gix[:, b, 1:2], axis=0),
                    bounds_check=NT * P - 1, oob_is_err=False).then_inc(gs[b], 16)

            def give(b, n):
                nc.gpsimd.tensor_copy(oix[:, b:b + 1],
                                      TB[:, bass.ds(n, 1), 0:1].bitcast(i32).rearrange("p o f -> p (o f)")
                                      ).then_inc(o_ix, 1)
                pool.wait_ge(o_ix, n + 1)
                then_dma()
                nc.gpsimd.indirect_dma_start(
                    out=out_rows, out_offset=bass.IndirectOffsetOnAxis(ap=oix[:, b:b + 1], axis=0),
                    in_=og[b], in_offset=None,
                    bounds_check=NT * P - 1, oob_is_err=False).then_inc(o_out[b], 16)

            for n in range(4):
                gather_x(n, n)
            for q in range(NQ):
                pool.wait_ge(s_out[q], 16 * 8)
            for n in range(4):
                gather_s(n, n)

            def steps(i):
                for k in range(4):
                    n = i * 4 + k
                    if isinstance(n, int) and n == 0:
                        continue
                    pool.wait_ge(o_ready, n)
                    gather_x((k + 3) % 4, n + 3)
                    give((k + 3) % 4, n - 1)
                    gather_s((k + 3) % 4, n + 3)
            pool.wait_ge(eo_ready, 1)
            last = each_round(pool, steps)
            pool.wait_ge(o_ready, last * 4 + 4)
            give(3, last * 4 + 3)
            for b in range(4):
                pool.wait_ge(o_out[b], last * 16 + 16)
                for gathered in (gx[b], gs[b]):
                    pool.wait_ge(gathered, last * 16 + (32 if b < 3 else 16))

        @block.scalar
        def _(act):

            def taps(j, u, i):
                act.wait_ge(pk_done, j + 1)
                need(act, ks_out[u], i * 16)
                nc.scalar.activation(kS[u], bank[2 + u][0:GC, :].rearrange("p (g j) -> p g j", g=4),
                                     ACT.Copy).then_inc(ks_ev, 1)

            def root(i):
                act.wait_ge(st_ready, i + 1)
                nc.scalar.activation(sd[:], ve[:], ACT.Sqrt).then_inc(sd_ready, 1)

            def turned(t, b):
                act.wait_ge(xT_done, t + 1)
                need(act, gate_done, t - 1)
                nc.scalar.activation(xnT[b], bank[b][:, :], ACT.Copy).then_inc(xT_ev, 1)

            def logits(n, u):
                if isinstance(n, int) and n == 0:
                    act.wait_ge(s_tab, 16)
                act.wait_ge(gate_done, n * 2 + 2)
                need(act, lg_done, n - 1)
                nc.scalar.activation(lgS[u], bank[4 + u][0:NE, 0:2 * P], ACT.Copy).then_inc(lg_ev, 1)

            def norm(i, with_taps=False):
                act.wait_ge(tk_ready, i + 1)
                for k in range(4):
                    t = i * 4 + k
                    need(act, xT_done, t - 3)
                    tile = XN[:, :, bass.ds(t, 1), :].rearrange("p q o d -> p q (o d)")
                    nc.scalar.activation(xnb[k].rearrange("p (q d) -> p q d", q=NQ), tile, ACT.Identity,
                                         bias=TOK[:, bass.ds(t, 1), 4], scale=TOK[:, bass.ds(t, 1), 5]
                                         ).then_inc(xn_norm, 1)
                    first = isinstance(i, int) and i == 0
                    if k % 2 == 1 and not (first and k == 1):
                        logits(i * 2 + (k // 2 - 1), 1 - k // 2)
                    if not (first and k == 0):
                        turned(i * 4 + (k - 1), (k - 1) % 2)
                    if k == 0 and not (isinstance(i, int) and i == NT // 4 - 1):
                        root(i + 1)
                    if with_taps and k % 2 == 1:
                        taps(i * 2 + (k // 2 - 2 * TAPS_AT), k // 2, i - TAPS_AT)
            act.wait_ge(s_par, 32)
            nc.scalar.activation(SG, PW[:, 0:2], ACT.Sigmoid).then_inc(s_sig, 1)
            root(0)
            looped(act, 0, TAPS_AT, norm)
            looped(act, TAPS_AT, TAPS_AT + 8, lambda i: norm(i, True))
            looped(act, TAPS_AT + 8, NT // 4 - 1, norm, peel=0)
            norm(NT // 4 - 1)

            def v_out(b, g):
                act.wait_ge(vt_done, g + 1)
                need(act, s1_done, g - 1)
                for o in range(2):
                    half = slice(o * NS, (o + 1) * NS)
                    nc.scalar.activation(V[:, b, o].rearrange("p (h r) -> p h r", r=2 * NS)[:, :, half],
                                         bank[b][:, 0:P].rearrange("p (h r) -> p h r", r=2 * NS)[:, :, half],
                                         ACT.Copy).then_inc(v_ev, 1)

            def group_of(g):
                return XN[:, bass.ds(g // GPQ, 1), :, bass.ds(g % GPQ * GC, GC)].rearrange("p o t d -> p (o t) d")

            def power_copy(b, g):
                need(act, s2_done, g - 3)
                nc.scalar.activation(Rg[:, b], R[:, bass.ds(g, 1), :].rearrange("p o j -> p (o j)"), ACT.Copy
                                     ).then_inc(rg_ready, 1)

            def x_copy(b, g):
                need(act, t_done, g - 1)
                nc.scalar.activation(Xg[:, b], group_of(g).rearrange("p t d -> p d t"), ACT.Copy).then_inc(xg_ready, 1)

            def s_back(b, g):
                act.wait_ge(xn_placed, NT)
                act.wait_ge(s2_done, g + 1)
                nc.scalar.activation(group_of(g), bank[4 + b][:, :].rearrange("p (d t) -> p t d", d=GC),
                                     ACT.Copy).then_inc(o_ev, 1)

            act.wait_ge(w_free, 4 * NE)
            for g in range(3):
                power_copy(g, g)
            turned(NT - 1, 1)
            act.wait_ge(xn_placed, NT)
            for g in range(2):
                x_copy(g, g)
            act.wait_ge(kz_out, 32)
            v_out(0, 0)
            logits(NT // 2 - 1, 1)

            def high_part(e, c):
                act.wait_ge(st_in[c // 2], e * 16 + 16)
                nc.scalar.activation(W16[:, bass.ds(e, 1), 0, c].rearrange("p o h -> p (o h)"), stage[:, c],
                                     ACT.Copy, scale=scl[:, 2:3]).then_inc(hi_ready, 1)

            def conv(i, split=False):
                for k in range(4):
                    g = i * 4 + k
                    if split:
                        high_part(i - NG // 8, k)
                    left = NG - 1 - g if isinstance(g, int) else NG
                    if left >= 1:
                        v_out((k + 1) % 2, g + 1)
                    if left >= 3:
                        power_copy((k + 3) % 4, g + 3)
                    if left >= 2:
                        x_copy(k % 2, g + 2)
                    s_back(k % 2, g)
            conv(0)
            act.wait_ge(m_ready, 1)
            nc.scalar.activation(ra[:, 4, :], ra[:, 3, :], ACT.Exp).then_inc(e_ready, 1)
            looped(act, 1, NG // 8, conv, peel=0)
            act.wait_ge(scl_ready, 1)
            for q in (0, 1):
                act.wait_ge(s_out[q], 16 * 8)
                looped(act, NG // 8 + 4 * q, NG // 8 + 4 * q + (4 if q == 0 else 3), lambda i: conv(i, True), peel=0)
            conv(NG // 4 - 1, True)

            act.wait_ge(s_tab, 32)
            act.wait_ge(o_ev, NG)

            def norm3(b, n, i):
                act.wait_ge(gx[b], i * 16 + 16)
                need(act, x3_done, n - 1)
                nc.scalar.activation(xm[b % 2], xg[b], ACT.Identity, bias=TB[:, bass.ds(n, 1), 4],
                                     scale=TB[:, bass.ds(n, 1), 5]).then_inc(xm_ready, 1)

            def high_x(b, n):
                act.wait_ge(x3_done, n + 1)
                need(act, mm_done, n - 1)
                nc.scalar.activation(xmT[b][:, 0], bank[b][:, :], ACT.Copy, scale=XS).then_inc(xhi_ready, 1)

            def biases(b, n):
                experts = experts_of(act, n)
                need(act, t_half, n - 1)
                for f, e, to in zip((2, 3), experts, (ba[b], bb[b])):
                    last = nc.scalar.activation(to, BE[:, bass.ds(e, 1), :].rearrange("p o h -> p (o h)"), ACT.Copy,
                                                scale=TB[:, bass.ds(n, 1), f])
                last.then_inc(b_ready, 1)

            def silu(b, n):
                act.wait_ge(t_ready, n + 1)
                need(act, o_ready, n - 1)
                nc.scalar.activation(gg[b], tt[b], ACT.Silu).then_inc(g_ready, 1)

            norm3(0, 0, 0)
            norm3(1, 1, 0)
            high_x(0, 0)
            act.wait_ge(s_be, 16)

            def steps(i):
                for k in range(4):
                    n = i * 4 + k
                    high_x((k + 1) % 2, n + 1)
                    biases(k % 2, n)
                    if not (isinstance(n, int) and n == 0):
                        silu((k + 1) % 2, n - 1)
                    norm3((k + 2) % 4, n + 2, i + (k + 2) // 4)
            last = each_round(act, steps)
            silu(1, last * 4 + 3)

        @block.vector
        def _(v):
            V_ = nc.vector

            def stats(i):
                for k in range(4):
                    v.wait_ge(x_in[k], i * 16 + 16)
                    V_.bn_stats(bst[:, k], XN[:, :, bass.ds(i * 4 + k, 1), :].rearrange("p q o d -> p q (o d)"))

            def variance(i):
                v.drain()
                for k in range(4):
                    V_.bn_aggr(mv[:, k], bst[:, k])
                v.drain()
                V_.tensor_scalar(ve[:], mv[:, :, 1], EPS, None, ALU.add).then_inc(st_ready, 1)

            def invert(i):
                v.wait_ge(sd_ready, i + 1)
                V_.reciprocal(r0[:], sd[:])
                v.drain()
                V_.tensor_tensor(r1[:], r0[:], r0[:], ALU.mult)
                v.drain()
                V_.scalar_tensor_tensor(out=r1[:], in0=r1[:], scalar=-0.5, in1=ve[:], op0=ALU.mult, op1=ALU.mult)
                v.drain()
                V_.scalar_tensor_tensor(out=rs[:], in0=r1[:], scalar=1.5, in1=r0[:], op0=ALU.add, op1=ALU.mult)
                v.drain()
                V_.scalar_tensor_tensor(out=TOK[:, bass.ds(i * 4, 4), 4], in0=mv[:, :, 0], scalar=-1.0, in1=rs[:],
                                        op0=ALU.mult, op1=ALU.mult)
                V_.tensor_copy(TOK[:, bass.ds(i * 4, 4), 5], rs[:])
                v.drain().then_inc(tk_ready, 1)

            def chunk_maxima(i):
                for u in range(2):
                    v.wait_ge(w_in[u], i * 16 + 16)
                    V_.tensor_reduce(wmax[:, bass.ds(i * 2 + u, 1)], wch[u], AX.X, ALU.max,
                                     apply_absolute_value=True).then_inc(w_free, 1)

            def place(i):
                for k in range(4):
                    t = i * 4 + k
                    tile = XN[:, :, bass.ds(t, 1), :].rearrange("p q o d -> p q (o d)")
                    v.wait_ge(xn_norm, t + 1)
                    V_.tensor_scalar(tile, tile, TOK[:, bass.ds(t, 1), 5], TOK[:, bass.ds(t, 1), 4],
                                     ALU.mult, ALU.add).then_inc(xn_placed, 1)

            def norm(i):
                last = isinstance(i, int) and i == NT // 4 - 1
                if not last:
                    stats(i + 1)
                invert(i)
                if not last:
                    variance(i + 1)
                chunk_maxima(i)
                if not isinstance(i, int) or i > 0:
                    place(i - 1)
            stats(0)
            variance(0)
            v.wait_ge(s_tok, 16)
            looped(v, 0, NT // 4 - 1, norm)
            norm(NT // 4 - 1)
            place(NT // 4 - 1)

            v.wait_ge(xn_placed, NT)
            v.wait_ge(xT_done, NT)
            v.wait_ge(sc_zero, 1)
            v.drain()
            V_.tensor_reduce(scl[:, 0:1], wmax[:], AX.X, ALU.max)
            v.drain()
            V_.tensor_copy(spread, scl[:, 0:1].to_broadcast([P, P])).then_inc(wm_ready, 1)

            def carry(g, b):
                pS = bank[2 + b][:, 0:NT]
                v.wait_ge(s1_done, g + 1)
                for s in range(NB):
                    V_.tensor_tensor_scan(
                        SC[:, b, s, 1:TPB + 1], QP[:, 7, bass.ds(g, 1)].to_broadcast([P, TPB]),
                        pS[:, s * TPB:(s + 1) * TPB], 0.0, ALU.mult, ALU.add).then_inc(s_ext, 1)
                v.drain()
                need(v, s2_done, g - 1)
                V_.tensor_tensor(
                    rhs2[:, b].rearrange("p d (s t) -> p d s t", s=NB),
                    maskcq[:, bass.ds(g, 1), :].rearrange("p o d -> p (o d)").unsqueeze(2).unsqueeze(3)
                    .to_broadcast([P, GC, NB, TPB]),
                    SC[:, b, :, 0:TPB].unsqueeze(1).to_broadcast([P, GC, NB, TPB]), ALU.mult
                ).then_inc(rhs2_ready, 1)

            v.wait_ge(s_const, 16 * 6)

            bc = lambda a, n: a.unsqueeze(2).to_broadcast([P, NT, n])
            desc = col(C_DESC, NE).unsqueeze(1).to_broadcast([P, NT, NE])
            flat = lambda a: a.rearrange("p r t -> p (r t)")
            counts, scan = flat(CNT[:, :, :]), flat(SCAN)
            HALF = NPAIR * NT // 2

            def weight_scale():
                v.wait_ge(wm_done, 1)
                V_.tensor_reduce(scl[:, 0:1], bank[7][:, 0:P], AX.X, ALU.max)
                v.drain()
                V_.tensor_scalar(scl[:, 0:1], scl[:, 0:1], 2.0 ** -100, None, ALU.max)
                v.drain()
                V_.tensor_scalar(scl[:, 0:1].bitcast(i32), scl[:, 0:1].bitcast(i32), 0x7f800000, None, ALU.bitwise_and)
                v.drain()
                V_.tensor_scalar(scl[:, 1:2], scl[:, 0:1], 2.0 ** -12 / XS, None, ALU.mult)
                V_.tensor_scalar(scl[:, 3:4], scl[:, 0:1], 1.5 * 2.0 ** -13, None, ALU.mult)
                v.drain()
                V_.reciprocal(scl[:, 2:3], scl[:, 3:4])
                v.drain()
                V_.tensor_scalar(scl[:, 2:3].bitcast(i32), scl[:, 2:3].bitcast(i32), 0x7f800000, None, ALU.bitwise_and)
                v.drain().then_inc(scl_ready, 1)

            def low_part(e, c):
                v.wait_ge(hi_ready, e * 4 + (c + 1))
                V_.scalar_tensor_tensor(out=W16[:, bass.ds(e, 1), 1, c].rearrange("p o h -> p (o h)"),
                                        in0=stage[:, c], scalar=scl[:, 2:3],
                                        in1=W16[:, bass.ds(e, 1), 0, c].rearrange("p o h -> p (o h)"),
                                        op0=ALU.mult, op1=ALU.subtract).then_inc(lo_ready, 1)

            def logits():
                v.wait_ge(lg_done, NT // 2)
                V_.tensor_tensor(LG, pLG, bgs[:, :].unsqueeze(1).to_broadcast([P, NT, NE]), ALU.add)
                v.drain()

            def greatest(m):
                V_.tensor_reduce(ra[:, m], LG, AX.X, ALU.max)
                v.drain()
                V_.tensor_tensor(LQ, LG, bc(ra[:, m], NE), ALU.is_equal)
                v.drain()

            def lowest(r):
                V_.tensor_tensor(LQ, LQ, desc, ALU.mult)
                v.drain()
                V_.tensor_reduce(ra[:, r], LQ, AX.X, ALU.max)
                v.drain()

            def without(r):
                V_.tensor_tensor(LQ, desc, bc(ra[:, r], NE), ALU.is_equal)
                v.drain()
                V_.scalar_tensor_tensor(out=LG, in0=LQ, scalar=-3.0e38, in1=LG, op0=ALU.mult, op1=ALU.add)
                v.drain()

            def pair_number():
                V_.tensor_tensor(ra[:, 3], ra[:, 2], ra[:, 0], ALU.subtract).then_inc(m_ready, 1)
                V_.tensor_tensor(ra[:, 6], ra[:, 1], ra[:, 5], ALU.max)
                V_.tensor_tensor(ra[:, 7], ra[:, 1], ra[:, 5], ALU.min)
                v.drain()
                V_.tensor_tensor(ra[:, 2], ra[:, 1], ra[:, 5], ALU.is_gt)
                V_.tensor_scalar(ra[:, 0], ra[:, 6], -1.0, 8.0, ALU.mult, ALU.add)
                v.drain()
                V_.tensor_scalar(ra[:, 6], ra[:, 6], 1.0, 5.0, ALU.mult, ALU.add)
                V_.tensor_scalar(ra[:, 7], ra[:, 7], -1.0, 8.0, ALU.mult, ALU.add)
                v.drain()
                V_.tensor_tensor(ra[:, 6], ra[:, 6], ra[:, 0], ALU.mult)
                v.drain()
                V_.scalar_tensor_tensor(out=ra[:, 6], in0=ra[:, 6], scalar=0.5, in1=ra[:, 7],
                                        op0=ALU.mult, op1=ALU.add)
                v.drain()

            def one_hot(h):
                for u in range(2):
                    v.wait_ge(ks_out[u], 16 * 8)
                v.wait_ge(lg_done, NT // 2)
                t = slice(h * NT // 2, (h + 1) * NT // 2)
                V_.tensor_tensor(OH[:, t], col(C_PAIR, NPAIR).unsqueeze(1).to_broadcast([P, NT // 2, NPAIR]),
                                 ra[:, 6, t].unsqueeze(2).to_broadcast([P, NT // 2, NPAIR]), ALU.is_equal
                                 ).then_inc(oh_ready, 1)

            def weights():
                v.wait_ge(e_ready, 1)
                V_.tensor_scalar(ra[:, 0], ra[:, 4], 1.0, None, ALU.add)
                V_.tensor_scalar(ra[:, 1], ra[:, 2], -1.0, 1.0, ALU.mult, ALU.add)
                v.drain()
                V_.reciprocal(ra[:, 5], ra[:, 0])
                v.drain()
                V_.tensor_tensor(ra[:, 4], ra[:, 4], ra[:, 5], ALU.mult)
                v.drain()

            def weight(f):
                k1, k2 = ((2, 1), (1, 2))[f]
                V_.tensor_tensor(ra[:, 0], ra[:, 5], ra[:, k1], ALU.mult)
                V_.tensor_tensor(ra[:, 3], ra[:, 4], ra[:, k2], ALU.mult)
                v.drain()
                V_.tensor_tensor(TOK[:, :, 2 + f], ra[:, 0], ra[:, 3], ALU.add)
                v.drain()
                V_.tensor_scalar(TOK[:, :, 6 + f], TOK[:, :, 2 + f], scl[:, 1:2], None, ALU.mult)

            def count(c):
                v.wait_ge(cnt_done, c + 1)
                V_.tensor_copy(CNT[:, :, 16 * c:16 * c + 16],
                               bank[7 - c % 2][:, 0:16 * NPAIR].rearrange("p (t r) -> p r t", r=NPAIR)
                               ).then_inc(cnt_ev, 1)
                v.drain()

            def running(h):
                V_.tensor_tensor_scan(scan[:, h * HALF:(h + 1) * HALF], col(C_ONE).to_broadcast([P, HALF]),
                                      counts[:, h * HALF:(h + 1) * HALF],
                                      scan[:, HALF - 1:HALF] if h else 0.0, ALU.mult, ALU.add)
                v.drain()

            def before_tile():
                V_.tensor_tensor(scan, scan, counts, ALU.subtract)
                v.drain()

            def slots():
                V_.tensor_tensor(pr28[:, 0].unsqueeze(2), SCAN[:, :, NT - 1:NT], CNT[:, :, NT - 1:NT], ALU.add)
                v.drain()
                V_.scalar_tensor_tensor(out=pr28[:, 0].unsqueeze(2), in0=pr28[:, 0].unsqueeze(2), scalar=P - 1.0,
                                        in1=SCAN[:, :, 0:1], op0=ALU.add, op1=ALU.subtract)
                v.drain()
                V_.tensor_copy(pr28[:, 1].bitcast(i32), pr28[:, 0])
                v.drain()
                V_.tensor_scalar(pr28[:, 1].bitcast(i32), pr28[:, 1].bitcast(i32), 7, 7,
                                 ALU.arith_shift_right, ALU.arith_shift_left)
                v.drain()
                V_.tensor_copy(pr28[:, 0], pr28[:, 1].bitcast(i32))
                v.drain()

            def starts():
                V_.tensor_tensor_scan(pr28[:, 2], col(C_ONE).to_broadcast([P, NPAIR]), pr28[:, 0], 0.0,
                                      ALU.mult, ALU.add)
                v.drain()
                V_.tensor_copy(last_round[:], pr28[:, 2, NPAIR - 1:NPAIR])
                V_.tensor_tensor(pr28[:, 3], pr28[:, 2], pr28[:, 0], ALU.subtract)
                v.drain()
                V_.tensor_tensor(pr28[:, 3].unsqueeze(2), pr28[:, 3].unsqueeze(2), SCAN[:, :, 0:1], ALU.subtract)
                V_.tensor_scalar(last_round[:], last_round[:], -1, None, ALU.add)
                v.drain()
                V_.tensor_scalar(last_round[:], last_round[:], 9, None, ALU.arith_shift_right)
                v.drain()

            def first_slot():
                V_.tensor_tensor(SCAN, SCAN, pr28[:, 3].unsqueeze(2).to_broadcast([P, NPAIR, NT]), ALU.add)
                v.drain()

            def experts():
                for f, c in enumerate((C_DA, C_DB)):
                    V_.scalar_tensor_tensor(out=pr28[:, 4 + f], in0=pr28[:, 2], scalar=col(C_IOTA), in1=col(c, NPAIR),
                                            op0=ALU.is_le, op1=ALU.mult)
                v.drain()
                for f in range(2):
                    V_.tensor_reduce(AB[:, f:f + 1], pr28[:, 4 + f], AX.X, ALU.add)
                v.drain()
                V_.tensor_scalar(AB[:, 1:2], AB[:, 1:2], 1.0, None, ALU.add)
                v.drain()
                V_.scalar_tensor_tensor(out=AB[:, 0:1], in0=AB[:, 0:1], scalar=float(NE), in1=AB[:, 1:2],
                                        op0=ALU.mult, op1=ALU.add)
                v.drain().then_inc(ab_ready, 1)

            def slot(c):
                v.wait_ge(pre_done, c + 1)
                V_.tensor_tensor(TMP, bank[7 - c % 2][:, 0:16 * NPAIR].rearrange("p (t r) -> p t r", r=NPAIR),
                                 SCAN[:, :, 16 * c:16 * c + 16].rearrange("p r t -> p t r"), ALU.add
                                 ).then_inc(pre_ev, 1)
                v.drain()
                V_.tensor_tensor(TMP, TMP, OH[:, 16 * c:16 * c + 16], ALU.mult)
                v.drain()
                V_.tensor_reduce(SLF[:, 16 * c:16 * c + 16], TMP, AX.X, ALU.add)
                v.drain()

            def table_rows():
                n, m = ra[:, 0].bitcast(i32), ra[:, 1].bitcast(i32)
                V_.tensor_copy(n, SLF)
                v.drain()
                V_.tensor_scalar(m, n, 7, None, ALU.arith_shift_right)
                V_.tensor_scalar(n, n, P - 1, None, ALU.bitwise_and)
                v.drain()
                V_.tensor_copy(ra[:, 2], n)
                V_.tensor_copy(ra[:, 3], m)
                v.drain()
                V_.scalar_tensor_tensor(out=ra[:, 4], in0=ra[:, 2], scalar=float(NX), in1=ra[:, 3],
                                        op0=ALU.mult, op1=ALU.add)
                v.drain()
                V_.tensor_copy(SLOT[:], ra[:, 4])
                v.drain().then_inc(slot_ready, 1)

            def tile_experts():
                v.wait_ge(eo_done, 1)
                V_.tensor_copy(EO[:], bank[6][0:1, 0:P]).then_inc(eo_ready, 1)

            g = 0

            def then(*parts):
                nonlocal g
                carry(g, g % 2)
                g += 1
                for part, *args in parts:
                    part(*args)

            then((logits,), (greatest, 0))
            then((lowest, 1), (weight_scale,))
            then((without, 1), (greatest, 2))
            then((lowest, 5), (pair_number,))
            then((one_hot, 0), (one_hot, 1))
            then((weights,), (weight, 0), (weight, 1))
            then((count, 0), (count, 1))
            then((count, 2), (count, 3))
            then((running, 0), (running, 1))
            then((before_tile,))
            then((slots,), (starts,))
            then((first_slot,))
            for c in range(4):
                then((slot, c))
            then((table_rows,))
            then((experts,))
            then()
            then()
            then((tile_experts,))
            while g < 24:
                then()
            with v.Fori(6, NG // 8) as i:
                for k in range(4):
                    carry(i * 4 + k, k % 2)
            with v.Fori(0, NE) as e:
                for k in range(4):
                    carry(e * 4 + (NG // 2 + k), k % 2)
                    low_part(e, k)

            v.wait_ge(s_tab, 32)
            v.wait_ge(o_ev, NG)

            def low_x(b, n):
                v.wait_ge(xhi_ready, n + 1)
                V_.scalar_tensor_tensor(out=xmT[b][:, 1], in0=bank[b][:, :], scalar=XS, in1=xmT[b][:, 0],
                                        op0=ALU.mult, op1=ALU.subtract).then_inc(xlo_ready, 1)

            def bias(b, n):
                v.wait_ge(b_ready, n + 1)
                V_.tensor_tensor(ba[b], ba[b], bb[b], ALU.add).then_inc(b_used, 1)

            def combine_a(b, n):
                v.wait_ge(b_used, n + 1)
                v.wait_ge(mm_done, n + 1)
                need(v, g_ready, n - 1)
                V_.scalar_tensor_tensor(out=tt[b], in0=bank[2 + b][:, :], scalar=TB[:, bass.ds(n, 1), 6], in1=ba[b],
                                        op0=ALU.mult, op1=ALU.add).then_inc(t_half, 1)

            def combine_b(b, n):
                v.wait_ge(t_half, n + 1)
                V_.scalar_tensor_tensor(out=tt[b], in0=bank[4 + b][:, :], scalar=TB[:, bass.ds(n, 1), 7], in1=tt[b],
                                        op0=ALU.mult, op1=ALU.add).then_inc(t_ready, 1)

            def final(b, n, i):
                v.wait_ge(gs[b], i * 16 + 16)
                v.wait_ge(g_ready, n + 1)
                V_.tensor_tensor(gg[b % 2], gg[b % 2], sg[b], ALU.mult)
                v.drain()
                need(v, o_out[b], i * 16)
                V_.tensor_tensor(og[b], gg[b % 2], xg[b], ALU.add).then_inc(o_ready, 1)

            low_x(0, 0)

            def steps(i):
                for k in range(4):
                    n = i * 4 + k
                    first = isinstance(n, int) and n == 0
                    if not first:
                        combine_a((k + 1) % 2, n - 1)
                    low_x((k + 1) % 2, n + 1)
                    if not first:
                        combine_b((k + 1) % 2, n - 1)
                    bias(k % 2, n)
                    if not first:
                        final((k + 3) % 4, n - 1, i if k > 0 else i - 1)
            last = each_round(v, steps)
            combine_a(1, last * 4 + 3)
            combine_b(1, last * 4 + 3)
            final(3, last * 4 + 3, last)

        @block.tensor
        def _(pe):
            ident = col(C_ID, P)
            pe.wait_ge(s_const, 16 * 6)

            def taps(j, u):
                pe.wait_ge(cm_ready, j + 1)
                need(pe, ks_ev, j - 1)
                for k in range(4):
                    last = nc.tensor.matmul(bank[2 + u][0:GC, k * P:(k + 1) * P], cmg[:, u, k],
                                            R[:, bass.ds(j * 4 + k, 1), :].rearrange("p o j -> p (o j)"),
                                            start=True, stop=True)
                last.then_inc(pk_done, 1)

            def turn(t, b):
                pe.wait_ge(xn_norm, t + 1)
                need(pe, xT_ev, t - 1)
                for c in range(NQ):
                    last = nc.tensor.transpose(bank[b % 2][:, c * P:(c + 1) * P], xnb[b][:, c * P:(c + 1) * P], ident)
                last.then_inc(xT_done, 1)

            def gate(t, b, n, u, k):
                pe.wait_ge(xT_ev, t + 1)
                if k == 0:
                    need(pe, lg_ev, n - 1)
                for c in range(NQ):
                    last = nc.tensor.matmul(bank[4 + u][0:NE, k * P:(k + 1) * P], wg[:, c],
                                            xnT[b][:, c * P:(c + 1) * P], start=(c == 0), stop=(c == NQ - 1))
                last.then_inc(gate_done, 1)

            def gate_turn(n, u):
                pe.wait_ge(lg_ev, n + 1)
                for k in range(2):
                    last = nc.tensor.matmul(bank[6][:, bass.ds(n * 2 * NE + k * NE, NE)], lgS[u][:, k * P:(k + 1) * P],
                                            ident[0:NE, 0:NE], start=True, stop=True)
                last.then_inc(lg_done, 1)

            def norm(i, with_taps=False):
                first = isinstance(i, int) and i == 0
                for k in range(4):
                    turn(i * 4 + k, k)
                    if not (first and k == 0):
                        gate(i * 4 + (k - 1), (k - 1) % 2, i * 2 + (k + 1) // 2 - 1, (k + 1) // 2 % 2 ^ 1, (k - 1) % 2)
                    if k % 2 == 1 and not (first and k == 1):
                        gate_turn(i * 2 + (k // 2 - 1), 1 - k // 2)
                    if with_taps and k % 2 == 0:
                        taps(i * 2 + (k // 2 - 2 * TAPS_AT), k // 2)
            looped(pe, 0, TAPS_AT, norm)
            looped(pe, TAPS_AT, TAPS_AT + 8, lambda i: norm(i, True), peel=1)
            looped(pe, TAPS_AT + 8, NT // 4, norm, peel=0)

            def v_turn(g, k):
                pe.wait_ge(rg_ready, g + 1)
                need(pe, v_ev, g * 2 - 2)
                nc.tensor.transpose(bank[k % 2][:, 0:P], Rg[:, k], ident).then_inc(vt_done, 1)

            def states(g, k):
                pe.wait_ge(xg_ready, g + 1)
                pe.wait_ge(v_ev, g * 2 + 2)
                need(pe, s_ext, g * 2 - 2)
                for h in range(4):
                    for o in range(2):
                        last = nc.tensor.matmul(bank[2 + k % 2][32 * h:32 * h + 32, 0:NT],
                                                V[:, k % 2, o, 32 * h:32 * h + 32], Xg[:, k % 2, 2 * h + o],
                                                start=(o == 0), stop=(o == 1))
                last.then_inc(s1_done, 1)

            def within(g, k, i):
                pe.wait_ge(t_in[k % 2], i * 32 + 16 * (k // 2 + 1))
                need(pe, o_ev, g - 1)
                for c in range(GC):
                    last = nc.tensor.matmul(bank[4 + k % 2][:, c * NT:(c + 1) * NT], Tb[:, k % 2, c], Xg[:, k % 2, c],
                                            start=(c == 0), stop=False)
                last.then_inc(t_done, 1)

            def before(g, k):
                pe.wait_ge(rhs2_ready, g + 1)
                nc.tensor.matmul(bank[4 + k % 2][:, :], Rg[:, k], rhs2[:, k % 2].rearrange("p d t -> p (d t)"),
                                 start=False, stop=True).then_inc(s2_done, 1)

            def conv(i):
                for k in range(4):
                    g = i * 4 + k
                    more = not (isinstance(g, int) and g == NG - 1)
                    if more:
                        v_turn(g + 1, (k + 1) % 4)
                    within(g, k, i)
                    if more:
                        states(g + 1, (k + 1) % 4)
                    before(g, k)
                    if isinstance(g, int):
                        after(g)

            oh = OH.rearrange("p t r -> p (t r)")

            def pairs(c, weights, done):
                nc.tensor.matmul(bank[7 - c % 2][:, 0:16 * NPAIR], weights[:],
                                 oh[:, c * 16 * NPAIR:(c + 1) * 16 * NPAIR], start=True, stop=True).then_inc(done, 1)

            def after(g):
                if g == 0:
                    pe.wait_ge(wm_ready, 1)
                    nc.tensor.matmul(bank[7][:, 0:P], spread, ident, start=True, stop=True).then_inc(wm_done, 1)
                for c in {5: (0, 1), 6: (2, 3)}.get(g, ()):
                    pe.wait_ge(oh_ready, 2)
                    need(pe, cnt_ev, c - 1)
                    pairs(c, ones16, cnt_done)
                for c in {10: (0, 1), 13: (2,), 14: (3,)}.get(g, ()):
                    pe.wait_ge(cnt_ev, 4)
                    need(pe, pre_ev, c - 1)
                    pairs(c, tri16, pre_done)
                if g == 19:
                    pe.wait_ge(ab_ready, 1)
                    pe.wait_ge(pre_ev, 4)
                    nc.tensor.matmul(bank[6][0:1, 0:P], AB[:, 0:1], ident, start=True, stop=True).then_inc(eo_done, 1)

            v_turn(0, 0)
            gate(NT - 1, 1, NT // 2 - 1, 1, 1)
            states(0, 0)
            gate_turn(NT // 2 - 1, 1)
            for i in range(5):
                conv(i)
            looped(pe, 5, NG // 4 - 1, conv, peel=0)
            conv(NG // 4 - 1)

            def turn3(n, b):
                pe.wait_ge(xm_ready, n + 1)
                need(pe, xlo_ready, n - 1)
                for c in range(NQ):
                    last = nc.tensor.transpose(bank[b][:, c * P:(c + 1) * P], xm[b][:, c * P:(c + 1) * P], ident)
                last.then_inc(x3_done, 1)

            def products(n, b, ea, eb):
                pe.wait_ge(xlo_ready, n + 1)
                need(pe, t_ready, n - 1)
                for c in range(NQ):
                    for y, e in ((2, ea), (4, eb)):
                        for f in range(2):
                            nc.tensor.matmul(bank[y + b][:, :], xmT[b][:, 0, c * P:(c + 1) * P],
                                             W16[:, bass.ds(e, 1), f, c].rearrange("p o h -> p (o h)"),
                                             start=(c == 0 and f == 0), stop=False)
                    for y, e in ((2, ea), (4, eb)):
                        last = nc.tensor.matmul(bank[y + b][:, :], xmT[b][:, 1, c * P:(c + 1) * P],
                                                W16[:, bass.ds(e, 1), 0, c].rearrange("p o h -> p (o h)"),
                                                start=False, stop=(c == NQ - 1))
                last.then_inc(mm_done, 1)

            pe.wait_ge(lo_ready, NQ * NE)
            pe.wait_ge(eo_ready, 1)
            turn3(0, 0)

            def steps(i):
                for k in range(4):
                    n = i * 4 + k
                    ea, eb = experts_of(pe, n)
                    turn3(n + 1, (k + 1) % 2)
                    products(n, k % 2, ea, eb)
            each_round(pe, steps)


def constants():
    import numpy as np
    c = np.zeros((P, NCST), np.float32)
    p = np.arange(P)
    c[:, C_ID:C_ID + P] = np.eye(P)
    c[:, C_TRI:C_TRI + P] = p[:, None] < p[None, :]
    c[:, C_MASK:C_MASK + GC] = p[:, None] // NS == np.arange(GC)
    c[:, C_DESC:C_DESC + NE] = NE - np.arange(NE)
    pairs = [(a, b) for a in range(NE) for b in range(a + 1, NE)]
    c[:, C_PAIR:C_PAIR + NPAIR] = 1 + np.arange(NPAIR)
    for k, at in ((0, C_DA), (1, C_DB)):
        c[:, at:at + NPAIR - 1] = np.diff([pair[k] for pair in pairs])
    c[:, C_ONE] = 1
    c[:, C_E0] = p // NS % 2 == 0
    c[:, C_E1] = p // NS % 2 == 1
    c[:, C_IOTA] = p * P
    tok = np.zeros((P, NT, TF), np.int32)
    tok[:, :, 0] = np.arange(NT) * P + p[:, None]
    tok[:, :, 1] = np.arange(NT) * P + (P - 1 - p[:, None])
    return c, tok


def kernel(L0_attn_x, L0_attn_delta, L0_attn_alpha, L0_attn_beta, L0_attn_gamma, L0_attn_omega,
           L0_ffn_We, L0_ffn_be, L0_ffn_Wg, L0_ffn_bg):
    import numpy as np
    import concourse.bacc as bacc
    from concourse.bass_utils import run_bass_kernel_spmd as run

    states = lambda a: np.ascontiguousarray(np.asarray(a).reshape(NG, P).T)
    cst, tok = constants()
    arrays = {
        "x": np.ascontiguousarray(L0_attn_x),
        "delta": states(L0_attn_delta), "alpha": states(L0_attn_alpha),
        "beta": states(L0_attn_beta), "gamma": states(L0_attn_gamma),
        "omega": np.ascontiguousarray(np.asarray(L0_attn_omega).reshape(NG, GC).T),
        "weT": np.ascontiguousarray(np.asarray(L0_ffn_We).reshape(NE, D, NQ, P).transpose(3, 2, 0, 1)),
        "be": np.ascontiguousarray(L0_ffn_be),
        "wgT": np.ascontiguousarray(np.asarray(L0_ffn_Wg).reshape(NE, NQ, P).transpose(2, 1, 0)),
        "bg": np.ascontiguousarray(L0_ffn_bg),
        "cst": cst, "tok": tok,
    }
    nc = bacc.Bacc("TRN2", target_bir_lowering=False, num_devices=1)
    args = [nc.dram_tensor(f"in_{n}", a.shape, mybir.dt.from_np(a.dtype), kind="ExternalInput").ap()
            for n, a in arrays.items()]
    out = nc.dram_tensor("out", L0_attn_x.shape, mybir.dt.float32, kind="ExternalOutput").ap()
    program(nc, *args, out)
    r = run(nc, [{f"in_{n}": a for n, a in arrays.items()}], core_ids=[0])
    return r.results[0]["out"]
```
